# Optimizing a Trainium2 kernel written in Bass

```python
import numpy as np
import jax
import jax.numpy as jnp

def _softmax(x, axis=-1):
    return jax.nn.softmax(x, axis=axis)

def _gelu(x):
    return jax.nn.gelu(x, approximate=True)

def _silu(x):
    return jax.nn.silu(x)

def _sigmoid(x):
    return jax.nn.sigmoid(x)

def _layernorm(x, axis=-1, eps=1e-05):
    m = jnp.mean(x, axis=axis, keepdims=True)
    v = jnp.var(x, axis=axis, keepdims=True)
    return (x - m) / jnp.sqrt(v + eps)

def _scatter_add(tgt, idx, src, axis=0):
    return tgt.at[idx].add(src)

def _segment_sum(src, seg, n):
    return jax.ops.segment_sum(src, seg, n)
kernel_name = 'mk_xattn_seq_d1_seqx_r4_d6b856'

def setup_inputs(seed: int=0):
    np.random.seed(seed)
    _w = jnp.asarray

    def _rec_inputs():
        import jax
        import jax.numpy as jnp
        _rk = jax.random.key(seed)
        x = -0.000296 + 1 * jax.random.normal(jax.random.fold_in(_rk, 1), (16, 256, 320), jnp.float32)
        _lenS = 256 - jax.random.randint(jax.random.fold_in(_rk, 7), (16,), 0, max(1, 256 // 4) + 1, jnp.int32)
        _lenS2 = 256 - jax.random.randint(jax.random.fold_in(_rk, 8), (16,), 0, max(1, 256 // 4) + 1, jnp.int32)
        _ctx_2048P = jax.random.normal(jax.random.fold_in(_rk, 11), (16, 16, 512), jnp.float32)
        _ctx_2048c = jax.random.dirichlet(jax.random.fold_in(_rk, 511), 0.3 * jnp.ones((16,), jnp.float32), (16, 256))
        _ctx_2048t = jnp.einsum('bsk,bkd->bsd', _ctx_2048c, _ctx_2048P)
        _ctx_2048t = _ctx_2048t * jax.lax.rsqrt(jnp.mean(jnp.square(_ctx_2048t)) + 1e-12) * 0.953939
        ctx_2048 = 0.00118529 + 0.99962 * (_ctx_2048t + 0.3 * jax.random.normal(jax.random.fold_in(_rk, 611), (16, 256, 512), jnp.float32))
        fside_Bx4x4_0 = jax.random.uniform(jax.random.fold_in(_rk, 12), (16, 4, 4), jnp.float32, 0.0, 0.981965)
        return (x, ctx_2048, fside_Bx4x4_0)
    x, ctx_2048, fside_Bx4x4_0 = _rec_inputs()

    def _L0_xattn_setup():
        import jax, jax.numpy as jnp
        import numpy as np
        HEADS = 20
        NUM_IP_TOKENS = 4
        NUM_DUMMY_TOKENS = 4
        IP_SCALE = 1.0
        ASPECT_RATIO = 1.0
        NEG = -10000.0

        def _grid_hw(seq_len, aspect_ratio):
            width = int((seq_len / aspect_ratio) ** 0.5)
            height = seq_len // width
            while width * height != seq_len:
                if width * height < seq_len:
                    width += 1
                else:
                    width -= 1
                height = seq_len // width
            return (height, width)

        def _sdpa(q, k, v, mask=None):
            dh = q.shape[-1]
            scores = jnp.einsum('bhqd,bhkd->bhqk', q, k) / jnp.sqrt(jnp.asarray(dh, q.dtype))
            if mask is not None:
                scores = scores + mask
            probs = jax.nn.softmax(scores, axis=-1)
            return jnp.einsum('bhqk,bhkd->bhqd', probs, v)

        def _split_heads(x, heads):
            b, l, d = x.shape
            return x.reshape(b, l, heads, d // heads).transpose(0, 2, 1, 3)

        def _merge_heads(x):
            b, h, l, dh = x.shape
            return x.transpose(0, 2, 1, 3).reshape(b, l, h * dh)

        def _ip_mask(bbox, batch_size, seq_len, dtype):
            M = bbox.shape[1]
            height, width = _grid_hw(seq_len, ASPECT_RATIO)
            x = jnp.linspace(0.0, 1.0, width, dtype=dtype)
            y = jnp.linspace(0.0, 1.0, height, dtype=dtype)
            yg, xg = jnp.meshgrid(y, x, indexing='ij')
            xg = xg.reshape(-1)
            yg = yg.reshape(-1)
            x1, y1, x2, y2 = (bbox[..., 0:1], bbox[..., 1:2], bbox[..., 2:3], bbox[..., 3:4])
            inside = (xg >= x1) & (xg <= x2) & (yg >= y1) & (yg <= y2)
            ip_mask = jnp.where(inside, 0.0, NEG).astype(dtype)
            ip_mask = jnp.transpose(ip_mask, (0, 2, 1))[:, None]
            ip_mask = jnp.repeat(ip_mask, NUM_IP_TOKENS // M, axis=-1)
            dummy = jnp.where(jnp.any(inside, axis=1), NEG, 0.0).astype(dtype)
            dummy = jnp.repeat(dummy[:, None, :, None], NUM_DUMMY_TOKENS, axis=-1)
            return jnp.concatenate([dummy, ip_mask], axis=-1)
        key = jax.random.key(seed)
        ks = jax.random.split(key, 12)
        B, S, D, C = (4, 1024, 320, 512)
        text_len, M = (77, 4)
        hidden_states = jax.random.normal(ks[0], (B, S, D), jnp.float32)
        encoder_hidden_states = jax.random.normal(ks[1], (B, text_len + NUM_IP_TOKENS + NUM_DUMMY_TOKENS, C), jnp.float32)
        p1 = jax.random.uniform(ks[2], (B, M, 2), jnp.float32)
        p2 = jax.random.uniform(ks[3], (B, M, 2), jnp.float32)
        bbox = jnp.concatenate([jnp.minimum(p1, p2), jnp.maximum(p1, p2)], axis=-1)
        s = 0.02
        w_q = jax.random.normal(ks[4], (D, D), jnp.float32) * s
        w_k = jax.random.normal(ks[5], (C, D), jnp.float32) * s
        w_v = jax.random.normal(ks[6], (C, D), jnp.float32) * s
        w_k_ip = jax.random.normal(ks[7], (C, D), jnp.float32) * s
        w_v_ip = jax.random.normal(ks[8], (C, D), jnp.float32) * s
        w_out = jax.random.normal(ks[9], (D, D), jnp.float32) * s
        b_out = jnp.zeros((D,), jnp.float32)
        return {'hidden_states': hidden_states, 'encoder_hidden_states': encoder_hidden_states, 'bbox': bbox, 'w_q': w_q, 'w_k': w_k, 'w_v': w_v, 'w_k_ip': w_k_ip, 'w_v_ip': w_v_ip, 'w_out': w_out, 'b_out': b_out}
    _L0_xattn_all = _L0_xattn_setup()
    _L0_xattn_in = {k: v for k, v in _L0_xattn_all.items() if k in ('w_q', 'w_k', 'w_v', 'w_k_ip', 'w_v_ip', 'w_out', 'b_out')}
    del _L0_xattn_all
    return {'x': x, 'ctx_2048': ctx_2048, 'fside_Bx4x4_0': fside_Bx4x4_0, 'L0_xattn_w_q': _L0_xattn_in['w_q'], 'L0_xattn_w_k': _L0_xattn_in['w_k'], 'L0_xattn_w_v': _L0_xattn_in['w_v'], 'L0_xattn_w_k_ip': _L0_xattn_in['w_k_ip'], 'L0_xattn_w_v_ip': _L0_xattn_in['w_v_ip'], 'L0_xattn_w_out': _L0_xattn_in['w_out'], 'L0_xattn_b_out': _L0_xattn_in['b_out']}

def reference(x, ctx_2048, fside_Bx4x4_0, L0_xattn_w_q, L0_xattn_w_k, L0_xattn_w_v, L0_xattn_w_k_ip, L0_xattn_w_v_ip, L0_xattn_w_out, L0_xattn_b_out):
    import jax
    import jax.numpy as jnp

    def _L0_xattn_ref(hidden_states, encoder_hidden_states, bbox, w_q, w_k, w_v, w_k_ip, w_v_ip, w_out, b_out):
        import jax, jax.numpy as jnp
        import numpy as np
        HEADS = 20
        NUM_IP_TOKENS = 4
        NUM_DUMMY_TOKENS = 4
        IP_SCALE = 1.0
        ASPECT_RATIO = 1.0
        NEG = -10000.0

        def _grid_hw(seq_len, aspect_ratio):
            width = int((seq_len / aspect_ratio) ** 0.5)
            height = seq_len // width
            while width * height != seq_len:
                if width * height < seq_len:
                    width += 1
                else:
                    width -= 1
                height = seq_len // width
            return (height, width)

        def _sdpa(q, k, v, mask=None):
            dh = q.shape[-1]
            scores = jnp.einsum('bhqd,bhkd->bhqk', q, k) / jnp.sqrt(jnp.asarray(dh, q.dtype))
            if mask is not None:
                scores = scores + mask
            probs = jax.nn.softmax(scores, axis=-1)
            return jnp.einsum('bhqk,bhkd->bhqd', probs, v)

        def _split_heads(x, heads):
            b, l, d = x.shape
            return x.reshape(b, l, heads, d // heads).transpose(0, 2, 1, 3)

        def _merge_heads(x):
            b, h, l, dh = x.shape
            return x.transpose(0, 2, 1, 3).reshape(b, l, h * dh)

        def _ip_mask(bbox, batch_size, seq_len, dtype):
            M = bbox.shape[1]
            height, width = _grid_hw(seq_len, ASPECT_RATIO)
            x = jnp.linspace(0.0, 1.0, width, dtype=dtype)
            y = jnp.linspace(0.0, 1.0, height, dtype=dtype)
            yg, xg = jnp.meshgrid(y, x, indexing='ij')
            xg = xg.reshape(-1)
            yg = yg.reshape(-1)
            x1, y1, x2, y2 = (bbox[..., 0:1], bbox[..., 1:2], bbox[..., 2:3], bbox[..., 3:4])
            inside = (xg >= x1) & (xg <= x2) & (yg >= y1) & (yg <= y2)
            ip_mask = jnp.where(inside, 0.0, NEG).astype(dtype)
            ip_mask = jnp.transpose(ip_mask, (0, 2, 1))[:, None]
            ip_mask = jnp.repeat(ip_mask, NUM_IP_TOKENS // M, axis=-1)
            dummy = jnp.where(jnp.any(inside, axis=1), NEG, 0.0).astype(dtype)
            dummy = jnp.repeat(dummy[:, None, :, None], NUM_DUMMY_TOKENS, axis=-1)
            return jnp.concatenate([dummy, ip_mask], axis=-1)
        B, S, D = hidden_states.shape
        residual = hidden_states
        end_pos = encoder_hidden_states.shape[1] - (NUM_IP_TOKENS + NUM_DUMMY_TOKENS)
        text = encoder_hidden_states[:, :end_pos]
        ip_h = encoder_hidden_states[:, end_pos:]
        q = _split_heads(hidden_states @ w_q, HEADS)
        k = _split_heads(text @ w_k, HEADS)
        v = _split_heads(text @ w_v, HEADS)
        out_text = _sdpa(q, k, v)
        out_text = _merge_heads(out_text)
        mask_ip = _ip_mask(bbox, B, S, hidden_states.dtype)
        k_ip = _split_heads(ip_h @ w_k_ip, HEADS)
        v_ip = _split_heads(ip_h @ w_v_ip, HEADS)
        out_ip = _merge_heads(_sdpa(q, k_ip, v_ip, mask=mask_ip))
        out = out_text + IP_SCALE * out_ip
        out = out @ w_out + b_out
        out = out + residual
        return out
    x = _L0_xattn_ref(x, ctx_2048, fside_Bx4x4_0, L0_xattn_w_q, L0_xattn_w_k, L0_xattn_w_v, L0_xattn_w_k_ip, L0_xattn_w_v_ip, L0_xattn_w_out, L0_xattn_b_out)
    return x

_drawn_inputs = setup_inputs


def setup_inputs(seed=0):
    import zlib

    import numpy as np

    out = dict(_drawn_inputs(seed))
    spreads = {'L0_xattn_b_out': (0.0, 0.1)}
    factors = {'L0_xattn_w_q': 5.926, 'L0_xattn_w_k': 8.0, 'L0_xattn_w_k_ip': 6.595}
    for name, (base, spread) in spreads.items():
        noise = np.random.default_rng([zlib.crc32(name.encode()), seed]).standard_normal(out[name].shape)
        drawn = base * np.exp(spread * noise) if base else spread * noise
        out[name] = jnp.asarray(drawn.astype(out[name].dtype))
    for name, factor in factors.items():
        out[name] = (out[name] * factor).astype(out[name].dtype)
    return out
```

```python
import numpy as np
import concourse.bass as bass
from concourse import mybir
from contextlib import ExitStack

B, S, D, C = 16, 256, 320, 512
H, DH = 20, 16
NIP = 4
KEYS = 256
TEXT = KEYS - 2 * NIP
NSP = KEYS - TEXT
GRID = 16
NEG = -10000.0
PAIRS = H // 2
GB = 2
GROUPS = B // GB
GT = GB * S
QUADS = H // 4
SCALE = DH ** -0.5
P = 128
XC, CC = 3, C // P
MT_ROWS = [128, 128, 64]
VW = 2 * D
AUX = 9
HALF = PAIRS // 2


def xattn(nc, xT, ctxT, ctx_sp, bbox, wq, wk, wv, wk_ip, wv_ip, wo, bias, grid, ident, kaux, vones, outT):
    f32, f32r = mybir.dt.float32, mybir.dt.float32r
    ALU = mybir.AluOpType
    ACT = mybir.ActivationFunctionType
    AX = mybir.AxisListType

    q_parts = nc.dram_tensor("q_parts", [2, D, B * S], f32, kind="Internal").ap()
    k_parts = nc.dram_tensor("k_parts", [2, D, B * KEYS], f32, kind="Internal").ap()
    v_rows = nc.dram_tensor("v_rows", [B, 2, P, VW], f32, kind="Internal").ap()
    v_sp_rows = nc.dram_tensor("v_sp_rows", [B, NSP, VW], f32, kind="Internal").ap()
    aux_rows = nc.dram_tensor("aux_rows", [B, 32, S], f32, kind="Internal").ap()
    sum_rows = nc.dram_tensor("sum_rows", [2, 4, QUADS * 2 * S], f32, kind="Internal").ap()
    recip_rows = nc.dram_tensor("recip_rows", [2, 4, QUADS * 2 * S], f32, kind="Internal").ap()

    ctx = ExitStack()
    with ctx:
        def sb(name, shape, dt=f32):
            return ctx.enter_context(nc.sbuf_tensor(name, shape, dt))

        def sem(name):
            return ctx.enter_context(nc.semaphore(name))

        q_stack = sb("q_stack", [P, 2, PAIRS * S], f32r)
        k_stack = sb("k_stack", [P, 2, PAIRS * 2 * KEYS], f32r)
        probs = sb("probs", [P, 4, 4 * S])
        o_raw = sb("o_raw", [P, 2, QUADS * 2 * S])
        recips = sb("recips", [P, QUADS * 2 * S])
        sums = sb("sums", [P, QUADS * 2 * S // 32])
        sums_inv = sb("sums_inv", [P, QUADS * 2 * S // 32])
        o_norm = sb("o_norm", [P, QUADS, S])
        v_cur = sb("v_cur", [P, 2, 3, VW])
        x_res = sb("x_res", [P, 2, XC, S])
        out_sb = sb("out_sb", [P, XC, S])
        wo_sb = sb("wo_sb", [P, QUADS, D])
        bias_sb = sb("bias_sb", [P, XC])
        ident_sb = sb("ident_sb", [P, P])
        neg_max = sb("neg_max", [P, 2, 2, P])
        max_rows = sb("max_rows", [4 * PAIRS, S], f32r)

        x_hi = sb("x_hi", [P, XC, GT], f32r)
        x_lo = sb("x_lo", [P, 2, GT], f32r)
        wq_hi = sb("wq_hi", [P, XC, D], f32r)
        wq_lo = sb("wq_lo", [P, XC, D], f32r)
        wk_hl = sb("wk_hl", [P, 2, CC, D], f32r)
        wv_hl = sb("wv_hl", [P, 2, CC, D], f32r)
        qk_out = sb("qk_out", [P, 2, 2, GT], f32r)
        v_out = sb("v_out", [P, 2, VW])
        vsp_out = sb("vsp_out", [P, VW])
        text_mask = sb("text_mask", [P, 1])
        sp_ctx_hl = sb("sp_ctx_hl", [P, 2, CC, P], f32r)
        boxes = sb("boxes", [B, 16])
        zeros = sb("zeros", [B, S], f32r)
        flat_q = q_stack[:, :, :].rearrange("p a n -> p (a n)")
        c_hi = flat_q[:, 0:CC * GT].rearrange("p (c n) -> p c n", c=CC)
        c_lo = flat_q[:, CC * GT:2 * CC * GT].rearrange("p (c n) -> p c n", c=CC)
        wkip_hl = k_stack[:, 1, 0:2 * CC * D].rearrange("p (s c n) -> p s c n", s=2, c=CC)
        wvip_hl = k_stack[:, 1, 2 * CC * D:4 * CC * D].rearrange("p (s c n) -> p s c n", s=2, c=CC)
        flat_o = o_raw[:, :, :].rearrange("p a n -> p (a n)")
        x_raw = flat_o[:, 0:XC * GT].rearrange("p (c n) -> p c n", c=XC)
        c_raw = flat_o[:, XC * GT:(XC + CC) * GT].rearrange("p (c n) -> p c n", c=CC)
        wq_raw = flat_o[:, (XC + CC) * GT:(XC + CC) * GT + XC * D].rearrange("p (c n) -> p c n", c=XC)
        flat_p = probs[:, :, :].rearrange("p a n -> p (a n)")
        wkip_raw, wvip_raw, wk_raw = (
            flat_p[:, i * CC * D:(i + 1) * CC * D].rearrange("p (c n) -> p c n", c=CC) for i in range(3))
        wv_raw = recips[:, 0:CC * D].rearrange("p (c n) -> p c n", c=CC)
        sp_raw = recips[:, CC * D:CC * D + CC * P].rearrange("p (c n) -> p c n", c=CC)
        kaux_raw = recips[96:128, CC * (D + P):CC * (D + P) + 2 * KEYS]
        grid_sb = x_res[0:B, 0, 0:2, :]
        inside = x_res[0:B, 1, :, :]
        covered = x_res[0:B, 0, 2, :]
        mask_out = v_cur[0:B, 0, 0:2, :].rearrange("p k n -> p (k n)").rearrange(
            "p (j n) -> p j n", j=1 + NIP)

        def bank(name, n):
            return ctx.enter_context(nc.psum_tensor(name, [P, n * 512], f32))

        score_t = bank("score_t", 2)
        score_q = bank("score_q", 2)
        pv = [bank("pv0", 1), bank("pv1", 1)]
        pj = [bank("pj0", 1), bank("pj1", 1)]

        ksp_out = [score_t[:, 0:P], score_t[:, 512:512 + P], pv[0][:, 0:P]]

        ld = {n: sem("loaded_" + n) for n in ("sp", "wkip", "wvip", "wq", "wk", "wv", "small", "boxes")}
        w_high = sem("w_high")
        w_low = sem("w_low")
        x_loaded, c_loaded = sem("x_loaded"), sem("c_loaded")
        x_high, c_high = sem("x_high"), sem("c_high")
        x_split, c_split = sem("x_split"), sem("c_split")
        x_tail = sem("x_tail")
        tile_ready = sem("tile_ready")
        hi_done, lo_done = sem("hi_done"), sem("lo_done")
        v_evac = sem("v_evac")
        qk_stored = [sem("qk_stored0"), sem("qk_stored1")]
        v_stored = [sem("v_stored0"), sem("v_stored1")]
        ksp_ready, ksp_hi, ksp_lo = sem("ksp_ready"), sem("ksp_hi"), sem("ksp_lo")
        ksp_stored = [sem("ksp_stored0"), sem("ksp_stored1")]
        vsp_ready, vsp_done = sem("vsp_ready"), sem("vsp_done")
        sp_stored = sem("sp_stored")
        preset, mask_step, mask_done = sem("preset"), sem("mask_step"), sem("mask_done")
        kaux_step = sem("kaux_step")
        aux_stored = sem("aux_stored")
        stacks_set = sem("stacks_set")
        stack_loaded = [[sem(f"stack_loaded{a}{h}") for h in range(2)] for a in range(2)]
        v_loaded = [sem("v_loaded0"), sem("v_loaded1")]
        xr_loaded = [sem("xr_loaded0"), sem("xr_loaded1")]
        sq_ready, max_done = sem("sq_ready"), sem("max_done")
        tp_ready, rows_done = sem("tp_ready"), sem("rows_done")
        rows_loaded = [sem("rows_loaded0"), sem("rows_loaded1")]
        st_ready, exp_done = sem("st_ready"), sem("exp_done")
        pv_ready, o_evac = sem("pv_ready"), sem("o_evac")
        sums_stored, sums_loaded, inv_done, inv_stored, inv_loaded = (
            sem("sums_stored"), sem("sums_loaded"), sem("inv_done"), sem("inv_stored"), sem("inv_loaded"))
        scaled, o_ready = sem("scaled"), sem("o_ready")
        out_ready, out_done, out_stored = sem("out_ready"), sem("out_done"), sem("out_stored")

        def need(eng, s, value):
            if not isinstance(value, int) or value > 0:
                eng.wait_ge(s, value)

        def values_of(par, kind, h):
            return v_cur[:, par, kind, 2 * DH * h:2 * DH * (h + 1)]

        def halves(row):
            r = row.rearrange("p (h s n) -> p h s n", h=H, s=2)
            return r[:, :, 0, :], r[:, :, 1, :]

        def by_head(row):
            return row.rearrange("p (h n) -> p h n", h=H)

        def q_cols(par, p, a, n):
            return q_stack[:, par, p * S + a:p * S + a + n]

        def k_cols(par, p, head, tile, n):
            at = (2 * p + head) * KEYS + tile * P
            return k_stack[:, par, at:at + n]

        slot = lambda u, p: (PAIRS * u + p) % 4

        def batches(eng, body, last=B):
            for u in range(2):
                body(u, u)
            with eng.Fori(1, B // 2 - 1) as i:
                for u in range(2):
                    body(2 * i + u, u)
            for b in (B - 2, B - 1):
                body(b, b % 2)

        def groups(eng, body):
            body(0)
            with eng.Fori(1, GROUPS) as g:
                body(g)

        block = ctx.enter_context(nc.Block())

        @block.sync
        def _(sp):
            def rows(a):
                return a.rearrange("(c p) n -> p c n", p=P)

            def load_wq():
                sp.dma_start(wq_raw[:, 0:2, :], rows(wq[0:256, :])).then_inc(ld["wq"], 16)
                for at in (0, 64):
                    sp.dma_start(wq_raw[at:at + 64, 2, :], wq[256:320, :]).then_inc(ld["wq"], 16)

            sp.dma_start(sp_raw, rows(ctx_sp)).then_inc(ld["sp"], 16)
            sp.dma_start(wkip_raw, rows(wk_ip)).then_inc(ld["wkip"], 16)
            sp.dma_start(wvip_raw, rows(wv_ip)).then_inc(ld["wvip"], 16)
            load_wq()

            def load_group(g):
                need(sp, x_tail, g)
                cols = bass.ds(g * GT, GT)
                sp.dma_start(x_raw[:, 0:2, :], rows(xT[0:256, cols])).then_inc(x_loaded, 16)
                for at in (0, 64):
                    sp.dma_start(x_raw[at:at + 64, 2, :], xT[256:320, cols]).then_inc(x_loaded, 16)
                need(sp, c_split, g)
                sp.dma_start(c_raw, rows(ctxT[:, cols])).then_inc(c_loaded, 16)

            def store_group(g):
                for j in range(6):
                    m, r = j % 3, MT_ROWS[j % 3]
                    src = qk_out[0:r, j % 2, :, :].bitcast(f32)
                    sp.wait_ge(lo_done, 6 * g + j + 1)
                    for s in range(2):
                        if j < 3:
                            sp.dma_start(q_parts[s, m * P:m * P + r, bass.ds(g * GT, GT)], src[:, s, :])\
                                .then_inc(qk_stored[j % 2], 16)
                        else:
                            dst = k_parts[s].rearrange("p (b n) -> p b n", n=KEYS)[
                                m * P:m * P + r, bass.ds(g * GB, GB), 0:TEXT]
                            sp.dma_start(dst, src[:, s].rearrange("p (b n) -> p b n", b=GB)[:, :, 0:TEXT])\
                                .then_inc(qk_stored[j % 2], 16)
                for t in range(2 * GB):
                    sp.wait_ge(v_evac, 4 * g + t + 1)
                    dst = v_rows.rearrange("b k p n -> (b k) p n")[bass.ds(2 * GB * g + t, 1), :, :]
                    sp.dma_start(dst.rearrange("a p n -> (a p) n"), v_out[:, t % 2, :])\
                        .then_inc(v_stored[t % 2], 16)

            load_group(0)
            sp.dma_start(wk_raw, rows(wk)).then_inc(ld["wk"], 16)
            sp.dma_start(wv_raw, rows(wv)).then_inc(ld["wv"], 16)
            sp.dma_start(wo_sb[:, :, :], rows(wo)).then_inc(ld["small"], 16)
            sp.dma_start(bias_sb[:, :], bias).then_inc(ld["small"], 16)
            sp.dma_start(ident_sb[:, :], ident).then_inc(ld["small"], 16)
            with sp.Fori(1, GROUPS) as g:
                load_group(g)
                store_group(g - 1)
            store_group(GROUPS - 1)

            def load_stack(b, u, h):
                ps, n = h * HALF, HALF
                done = stack_loaded[u][h]
                cols = bass.ds(b * S, S)
                qv = q_stack[:, u, ps * S:(ps + n) * S].rearrange("p (a n) -> p a n", a=n).bitcast(f32)
                kv = k_stack[:, u, ps * 2 * KEYS:(ps + n) * 2 * KEYS].rearrange(
                    "p (a e n) -> p a e n", a=n, e=2).bitcast(f32)
                for quad, part in enumerate((0, 1, 0)):
                    src = q_parts[part, 32 * ps:32 * (ps + n), cols].rearrange("(a r) n -> r a n", r=32)
                    sp.dma_start(qv[32 * quad:32 * quad + 32, :, :], src).then_inc(done, 16)
                for quad, part in enumerate((0, 0, 1)):
                    src = k_parts[part, 32 * ps:32 * (ps + n), cols].rearrange(
                        "(a e r) n -> e r a n", e=2, r=DH)
                    for e in range(2):
                        at = 32 * quad + DH * e
                        sp.dma_start(kv[at:at + DH, :, e, :], src[e]).then_inc(done, 16)
                src = aux_rows[bass.ds(b, 1), :, :].rearrange("a r n -> (a r) n")
                sp.dma_start(qv[96:128, :, :], src.unsqueeze(1).broadcast_to([32, n, S])).then_inc(done, 16)

            def load_values(b, u):
                sp.dma_start(v_cur[:, u, 0:2, :], v_rows[bass.ds(b, 1), :, :, :].rearrange(
                    "a k p n -> (a p) k n")).then_inc(v_loaded[u], 16)
                sp.dma_start(v_cur[P - NSP:P, u, 2, :], v_sp_rows[bass.ds(b, 1), :, :].rearrange(
                    "a p n -> (a p) n")).then_inc(v_loaded[u], 16)

            def load_residual(b, u):
                cols = bass.ds(b * S, S)
                sp.dma_start(x_res[:, u, 0:2, :], rows(xT[0:256, cols])).then_inc(xr_loaded[u], 16)
                sp.dma_start(x_res[0:64, u, 2, :], xT[256:320, cols]).then_inc(xr_loaded[u], 16)

            for s in (0, 1):
                sp.wait_ge(qk_stored[s], 32 * 3 * GROUPS)
                sp.wait_ge(v_stored[s], 16 * 2 * GROUPS)
                sp.wait_ge(ksp_stored[s], 32 * (2 - s))
            sp.wait_ge(sp_stored, 16)
            sp.wait_ge(aux_stored, 48)
            sp.wait_ge(stacks_set, 2)
            sp.wait_ge(tile_ready, 10 * GROUPS)
            sp.wait_ge(mask_done, 1)
            for b in (0, 1):
                for h in range(2):
                    load_stack(b, b, h)
            load_values(0, 0)

            def batch(b, u):
                last = isinstance(b, int) and b == B - 1
                if not last:
                    need(sp, pv_ready, QUADS * b)
                    load_values(b + 1, 1 - u)
                if not (isinstance(b, int) and b >= B - 2):
                    for h in range(2):
                        need(sp, st_ready, PAIRS * b + (h + 1) * HALF)
                        load_stack(b + 2, u, h)
                if not (isinstance(b, int) and b < 2):
                    store_out(b - 2)
                load_residual(b, u)

            def store_out(b):
                need(sp, out_done, XC * (b + 1))
                cols = bass.ds(b * S, S)
                sp.dma_start(rows(outT[0:256, cols]), out_sb[:, 0:2, :]).then_inc(out_stored, 16)
                sp.dma_start(outT[256:320, cols], out_sb[0:64, 2, :]).then_inc(out_stored, 16)

            batches(sp, batch)
            for b in (B - 2, B - 1):
                store_out(b)
            sp.wait_ge(out_stored, 32 * B)

        @block.gpsimd
        def _(pool):
            pool.dma_start(boxes[:, :], bbox).then_inc(ld["boxes"], 16)
            pool.dma_start(grid_sb, grid).then_inc(ld["boxes"], 16)
            pool.dma_start(kaux_raw, kaux).then_inc(ld["boxes"], 16)
            pool.dma_start(text_mask[:, :], vones).then_inc(ld["boxes"], 16)
            pool.memset(zeros[:, :].bitcast(f32), 0.0).then_inc(preset, 1)
            pool.memset(v_cur[:, :, 2, :], 0.0).then_inc(preset, 1)
            pool.memset(halves(v_out[:, 0, :])[1], 1.0).then_inc(preset, 1)
            pool.memset(halves(vsp_out[:, :])[1], 1.0).then_inc(preset, 1)
            pool.memset(halves(v_out[:, 1, :])[1], 1.0).then_inc(preset, 1)
            pool.memset(neg_max[:, :, :, :], 0.0).then_inc(preset, 1)
            pool.memset(k_stack[0:96, 0, :].bitcast(f32), 0.0).then_inc(kaux_step, 1)
            pool.wait_ge(ld["boxes"], 64)
            pool.wait_ge(preset, 6)
            pool.tensor_scalar(halves(v_out[:, 1, :])[1], halves(v_out[:, 1, :])[1], text_mask[:, 0:1], None,
                               ALU.mult).then_inc(preset, 1)
            pool.dma_start(aux_rows[:, 0:4, :], zeros[:, :].bitcast(f32).unsqueeze(1).broadcast_to([B, 4, S])).then_inc(aux_stored, 16)
            pool.dma_start(aux_rows[:, AUX:32, :], zeros[:, :].bitcast(f32).unsqueeze(1).broadcast_to([B, 32 - AUX, S])).then_inc(aux_stored, 16)

            def constant_rows(u):
                pool.tensor_copy(
                    k_stack[96:128, u, :].rearrange("p (a n) -> p a n", a=PAIRS),
                    kaux_raw.unsqueeze(1).broadcast_to([32, PAIRS, 2 * KEYS])).then_inc(stacks_set, 1)

            for m, r in enumerate(MT_ROWS):
                pool.wait_ge(ksp_lo, m + 1)
                src = qk_out[0:r, m % 2, :, 0:P].rearrange("p s (b n) -> p s b n", b=B).bitcast(f32)
                dst = k_parts[:, m * P:m * P + r, :].rearrange("s p (b n) -> s p b n", b=B)
                for s in range(2):
                    pool.dma_start(dst[s, :, :, TEXT:KEYS], src[:, s]).then_inc(ksp_stored[m % 2], 16)
            pool.wait_ge(vsp_done, 1)
            pool.dma_start(v_sp_rows.rearrange("b p n -> (b p) n"), vsp_out[:, :]).then_inc(sp_stored, 16)

            pool.wait_ge(preset, 7)
            pool.wait_ge(kaux_step, 1)
            constant_rows(0)
            pool.wait_ge(vsp_ready, 1)
            pool.wait_ge(stacks_set, 1)
            pool.memset(k_stack[0:96, 1, :].bitcast(f32), 0.0).then_inc(kaux_step, 1)
            pool.wait_ge(kaux_step, 2)
            constant_rows(1)
            pool.wait_ge(mask_done, 1)
            pool.dma_start(aux_rows[:, 4:AUX, :], mask_out).then_inc(aux_stored, 16)

            def normalise(b, u):
                pool.wait_ge(inv_loaded, 16 * (b + 1))
                pool.tensor_tensor(o_raw[:, u, :], o_raw[:, u, :], recips[:, :], ALU.mult).then_inc(scaled, 1)
                pool.wait_ge(scaled, b + 1)
                need(pool, out_ready, XC * b)
                parts = o_raw[:, u, :].rearrange("p (k s n) -> p k s n", k=QUADS, s=2)
                pool.tensor_tensor(o_norm[:, :, :], parts[:, :, 0, :], parts[:, :, 1, :],
                                   ALU.add).then_inc(o_ready, 1)

            pool.wait_ge(stacks_set, 2)
            batches(pool, normalise)

        @block.scalar
        def _(act):
            def high(dst, src, loaded, value):
                act.wait_ge(loaded, value)
                nc.scalar.activation(dst, src, ACT.Copy).then_inc(w_high, 1)

            high(sp_ctx_hl[:, 0], sp_raw, ld["sp"], 16)
            high(wkip_hl[:, 0], wkip_raw, ld["wkip"], 16)
            high(wvip_hl[:, 0], wvip_raw, ld["wvip"], 16)
            high(wq_hi[:, :, :], wq_raw, ld["wq"], 48)

            def group(g):
                act.wait_ge(x_loaded, 48 * (g + 1))
                need(act, tile_ready, 10 * (g - 1) + 3)
                nc.scalar.activation(x_hi[:, :, :], x_raw, ACT.Copy).then_inc(x_high, 1)
                act.wait_ge(c_loaded, 16 * (g + 1))
                need(act, tile_ready, 10 * g)
                nc.scalar.activation(c_hi, c_raw, ACT.Copy).then_inc(c_high, 1)
                if isinstance(g, int) and g == 0:
                    high(wk_hl[:, 0], wk_raw, ld["wk"], 16)
                    high(wv_hl[:, 0], wv_raw, ld["wv"], 16)
                    act.wait_ge(ksp_stored[0], 64)
                    act.wait_ge(ksp_stored[1], 32)
                for j in range(6):
                    r = MT_ROWS[j % 3]
                    act.wait_ge(tile_ready, 10 * g + j + 1)
                    need(act, qk_stored[j % 2], 32 * (3 * g + j // 2))
                    nc.scalar.activation(qk_out[0:r, j % 2, 0, :], pj[j % 2][0:r, :], ACT.Copy)\
                        .then_inc(hi_done, 1)
                for t in range(4):
                    act.wait_ge(tile_ready, 10 * g + 7 + t)
                    need(act, v_stored[t % 2], 16 * (2 * g + t // 2))
                    if t % 2:
                        nc.scalar.activation(halves(v_out[:, 1, :])[0], by_head(pj[1][:, 0:D]), ACT.Copy,
                                             scale=text_mask[:, 0:1]).then_inc(v_evac, 1)
                    else:
                        nc.scalar.activation(halves(v_out[:, 0, :])[0], by_head(pj[0][:, 0:D]), ACT.Copy).then_inc(v_evac, 1)

            for m, r in enumerate(MT_ROWS):
                act.wait_ge(ksp_ready, m + 1)
                if m == 2:
                    act.wait_ge(ksp_stored[0], 32)
                nc.scalar.activation(qk_out[0:r, m % 2, 0, 0:P], ksp_out[m][0:r, :], ACT.Copy)\
                    .then_inc(ksp_hi, 1)
            act.wait_ge(vsp_ready, 1)
            nc.scalar.activation(halves(vsp_out[:, :])[0], by_head(score_q[:, 0:D]), ACT.Copy).then_inc(vsp_done, 1)
            act.wait_ge(preset, 7)
            groups(act, group)

            def max_to_rows(b, u):
                act.wait_ge(tp_ready, b + 1)
                need(act, rows_loaded[1 - u], 32 * (b + u))
                nc.scalar.activation(max_rows[:, :], pj[1][0:4 * PAIRS, 0:S], ACT.Copy).then_inc(rows_done, 1)
                act.wait_ge(rows_done, b + 1)
                for k in range(4):
                    act.dma_start(
                        q_stack[96 + k:97 + k, u, :].rearrange("p (a n) -> p a n", a=PAIRS).bitcast(f32),
                        max_rows[PAIRS * k:PAIRS * (k + 1), :].bitcast(f32)).then_inc(rows_loaded[u], 16)

            def reciprocals(b, u, step):
                if step == 0:
                    act.wait_ge(o_evac, QUADS * (b + 1))
                    act.dma_start(sum_rows[u], o_raw[DH:P:32, u, :]).then_inc(sums_stored, 16)
                elif step == 1:
                    act.wait_ge(sums_stored, 16 * (b + 1))
                    need(act, inv_done, b)
                    act.dma_start(sums[:, :], sum_rows[u].rearrange("t (a n) -> (t a) n", a=32))\
                        .then_inc(sums_loaded, 16)
                elif step == 2:
                    act.wait_ge(inv_done, b + 1)
                    act.dma_start(recip_rows[u].rearrange("t (a n) -> (t a) n", a=32), sums_inv[:, :])\
                        .then_inc(inv_stored, 16)
                else:
                    act.wait_ge(inv_stored, 16 * (b + 1))
                    need(act, scaled, b)
                    act.dma_start(recips[:, :], recip_rows[u].unsqueeze(1).broadcast_to(
                        [4, 32, QUADS * 2 * S])).then_inc(inv_loaded, 16)

            def batch(b, u):
                def evacuate(k):
                    n = QUADS * b + k
                    act.wait_ge(pv_ready, n + 1)
                    if k == 0:
                        need(act, o_ready, b - 1)
                    nc.scalar.activation(o_raw[:, u, k * 2 * S:(k + 1) * 2 * S], pv[(QUADS * u + k) % 2][:, :],
                                         ACT.Copy).then_inc(o_evac, 1)

                for p in range(PAIRS):
                    act.wait_ge(st_ready, PAIRS * b + p + 1)
                    need(act, pv_ready, QUADS * b + (p - 4) // 2 + 1)
                    nc.scalar.activation(probs[:, slot(u, p), :], score_t[:, :], ACT.Exp, scale=SCALE)\
                        .then_inc(exp_done, 1)
                    if p >= 2 and p % 2 == 0:
                        evacuate(p // 2 - 1)
                    if p in RECIP_STEPS and not (isinstance(b, int) and b == 0):
                        reciprocals(b - 1, 1 - u, RECIP_STEPS.index(p))
                    if p == TP_STEP and not (isinstance(b, int) and b == B - 1):
                        max_to_rows(b + 1, 1 - u)
                evacuate(QUADS - 1)

            max_to_rows(0, 0)
            batches(act, batch)
            for step in range(4):
                reciprocals(B - 1, 1, step)

        @block.vector
        def _(dve):
            steps = [0]

            def then(ins):
                steps[0] += 1
                ins.then_inc(mask_step, 1)
                dve.wait_ge(mask_step, steps[0])

            def mask():
                dve.wait_ge(ld["boxes"], 64)
                gx, gy = grid_sb[:, 0, :], grid_sb[:, 1, :]
                for j in range(NIP):
                    side = lambda c: boxes[:, 4 * j + c:4 * j + c + 1]
                    at = inside_j(j)
                    then(nc.vector.tensor_scalar(at, gx, side(0), None, ALU.is_ge))
                    for g, c, op in ((gx, 2, ALU.is_le), (gy, 1, ALU.is_ge), (gy, 3, ALU.is_le)):
                        then(nc.vector.scalar_tensor_tensor(out=at, in0=g, scalar=side(c), in1=at,
                                                            op0=op, op1=ALU.mult))
                    then(nc.vector.tensor_scalar(mask_out[:, 1 + j, :], at, -NEG / SCALE, NEG / SCALE,
                                                 ALU.mult, ALU.add))
                    if j == 0:
                        then(nc.vector.tensor_copy(covered, at))
                    else:
                        then(nc.vector.tensor_tensor(covered, covered, at, ALU.max))
                nc.vector.tensor_scalar(mask_out[:, 0, :], covered, NEG / SCALE, None, ALU.mult)\
                    .then_inc(mask_done, 1)

            def inside_j(j):
                return inside[:, j % 3, :]

            n_low = [0]

            def low(dst, raw, hi):
                n_low[0] += 1
                dve.wait_ge(w_high, n_low[0])
                nc.vector.tensor_tensor(dst, raw, hi.bitcast(f32), ALU.subtract).then_inc(w_low, 1)

            low(sp_ctx_hl[:, 1], sp_raw, sp_ctx_hl[:, 0])
            low(wkip_hl[:, 1], wkip_raw, wkip_hl[:, 0])
            low(wvip_hl[:, 1], wvip_raw, wvip_hl[:, 0])
            low(wq_lo[:, :, :], wq_raw, wq_hi[:, :, :])

            for m, r in enumerate(MT_ROWS):
                dve.wait_ge(ksp_hi, m + 1)
                if m == 2:
                    dve.wait_ge(ksp_stored[0], 32)
                nc.vector.tensor_tensor(qk_out[0:r, m % 2, 1, 0:P], ksp_out[m][0:r, :],
                                        qk_out[0:r, m % 2, 0, 0:P].bitcast(f32), ALU.subtract)\
                    .then_inc(ksp_lo, 1)

            def group(g):
                dve.wait_ge(x_high, g + 1)
                nc.vector.tensor_tensor(x_lo[:, :, :], x_raw[:, 0:2, :], x_hi[:, 0:2, :].bitcast(f32),
                                        ALU.subtract).then_inc(x_split, 1)
                nc.vector.tensor_tensor(x_hi[64:128, 2, :], x_raw[64:128, 2, :],
                                        x_hi[64:128, 2, :].bitcast(f32), ALU.subtract).then_inc(x_tail, 1)
                dve.wait_ge(c_high, g + 1)
                nc.vector.tensor_tensor(c_lo, c_raw, c_hi.bitcast(f32), ALU.subtract).then_inc(c_split, 1)
                if isinstance(g, int) and g == 0:
                    low(wk_hl[:, 1], wk_raw, wk_hl[:, 0])
                    low(wv_hl[:, 1], wv_raw, wv_hl[:, 0])
                for j in range(6):
                    r = MT_ROWS[j % 3]
                    dve.wait_ge(hi_done, 6 * g + j + 1)
                    nc.vector.tensor_tensor(qk_out[0:r, j % 2, 1, :], pj[j % 2][0:r, :],
                                            qk_out[0:r, j % 2, 0, :].bitcast(f32), ALU.subtract)\
                        .then_inc(lo_done, 1)
                if isinstance(g, int) and g == 0:
                    mask()

            groups(dve, group)

            def maxima(b, u, p):
                dve.wait_ge(sq_ready, PAIRS * b + p + 1)
                both = score_q[:, :].rearrange("p (t e n) -> p t e n", t=2, e=2)
                to = neg_max[:, u, :, 0:4 * PAIRS].rearrange("p t (k a) -> p t k a", k=4)
                nc.vector.tensor_reduce(out=to[:, :, 0:2, p], in_=both[:, :, :, 0:TEXT],
                                        op=ALU.max, axis=AX.X, negate=True)
                nc.vector.tensor_reduce(out=to[:, :, 2:4, p], in_=both[:, :, :, TEXT:KEYS],
                                        op=ALU.max, axis=AX.X, negate=True).then_inc(max_done, 1)

            def invert(b):
                dve.wait_ge(sums_loaded, 16 * (b + 1))
                need(dve, inv_stored, 16 * b)
                nc.vector.reciprocal(sums_inv[:, :], sums[:, :]).then_inc(inv_done, 1)

            def finish(b, u, m):
                r = MT_ROWS[m]
                dve.wait_ge(out_ready, XC * b + m + 1)
                if m == 0:
                    need(dve, out_stored, 32 * b)
                    dve.wait_ge(xr_loaded[u], 16 * (b - u) + 32)
                nc.vector.scalar_tensor_tensor(
                    out=out_sb[0:r, m, :], in0=pj[m % 2][0:r, 0:S], scalar=bias_sb[0:r, m:m + 1],
                    in1=x_res[0:r, u, m, :], op0=ALU.add, op1=ALU.add).then_inc(out_done, 1)

            dve.wait_ge(ld["small"], 48)
            for p in range(PAIRS):
                maxima(0, 0, p)

            def batch(b, u):
                first = isinstance(b, int) and b < 1
                for what, a in SCHEDULE:
                    if what == "max" and not (isinstance(b, int) and b == B - 1):
                        maxima(b + 1, 1 - u, a)
                    if what == "out" and not (isinstance(b, int) and b < 2):
                        finish(b - 2, u, a)
                    if what == "pv" and a == 1 and not first:
                        invert(b - 1)

            batches(dve, batch)
            for m in range(XC):
                finish(B - 2, 0, m)
            invert(B - 1)
            for m in range(XC):
                finish(B - 1, 1, m)

        @block.tensor
        def _(pe):
            mm = nc.tensor.matmul

            def three(out, w_hi, w_lo, x_hi_, x_lo_, start, stop):
                mm(out, w_hi, x_hi_, start=start, stop=False)
                mm(out, w_lo, x_hi_, start=False, stop=False)
                return mm(out, w_hi, x_lo_, start=False, stop=stop)

            pe.wait_ge(w_low, 2)
            for m, r in enumerate(MT_ROWS):
                for c in range(CC):
                    last = three(ksp_out[m][0:r, :], wkip_hl[:, 0, c, m * P:m * P + r],
                                 wkip_hl[:, 1, c, m * P:m * P + r], sp_ctx_hl[:, 0, c, :],
                                 sp_ctx_hl[:, 1, c, :], c == 0, c == CC - 1)
                last.then_inc(ksp_ready, 1)
            pe.wait_ge(w_low, 3)
            for c in range(CC):
                last = three(score_q[:, 0:D], sp_ctx_hl[:, 0, c, :], sp_ctx_hl[:, 1, c, :],
                             wvip_hl[:, 0, c, :], wvip_hl[:, 1, c, :], c == 0, c == CC - 1)
            last.then_inc(vsp_ready, 1)

            def group(g):
                first = isinstance(g, int) and g == 0
                if first:
                    pe.wait_ge(w_low, 4)
                pe.wait_ge(x_tail, g + 1)
                for j in range(6):
                    m, r = j % 3, MT_ROWS[j % 3]
                    out = pj[j % 2][0:r, :]
                    cols = slice(m * P, m * P + r)
                    if j < 2:
                        need(pe, v_evac, 4 * g - 1 + j)
                    else:
                        pe.wait_ge(lo_done, 6 * g + j - 1)
                    if j < 3:
                        for c in range(2):
                            three(out, wq_hi[:, c, cols], wq_lo[:, c, cols], x_hi[:, c, :], x_lo[:, c, :],
                                  c == 0, False)
                        mm(out, wq_hi[:, 2, cols], x_hi[:, 2, :], start=False, stop=False)
                        last = mm(out, wq_lo[:, 2, cols], x_hi[:, 2, :], start=False, stop=True)
                    else:
                        if j == 3:
                            pe.wait_ge(c_split, g + 1)
                            if first:
                                pe.wait_ge(w_low, 5)
                        for c in range(CC):
                            last = three(out, wk_hl[:, 0, c, cols], wk_hl[:, 1, c, cols], c_hi[:, c, :],
                                         c_lo[:, c, :], c == 0, c == CC - 1)
                    last.then_inc(tile_ready, 1)
                if first:
                    pe.wait_ge(w_low, 6)
                for t in range(2 * GB):
                    if t < 2:
                        pe.wait_ge(lo_done, 6 * g + 5 + t)
                    else:
                        pe.wait_ge(v_evac, 4 * g + t - 1)
                    keys = slice(t * P, t * P + P)
                    for c in range(CC):
                        last = three(pj[t % 2][:, 0:D], c_hi[:, c, keys], c_lo[:, c, keys],
                                     wv_hl[:, 0, c, :], wv_hl[:, 1, c, :], c == 0, c == CC - 1)
                    last.then_inc(tile_ready, 1)

            groups(pe, group)

            def query_scores(b, u, p):
                if p % HALF == 0:
                    pe.wait_ge(stack_loaded[u][p // HALF],
                               80 * (b - u) + 160)
                need(pe, max_done, PAIRS * b + p)
                for t in range(2):
                    last = mm(score_q[:, 512 * t:512 * t + 512], q_cols(u, p, t * P, P),
                              k_cols(u, p, 0, 0, 2 * KEYS), start=True, stop=True)
                last.then_inc(sq_ready, 1)

            def key_scores(b, u, p):
                if p == 0:
                    pe.wait_ge(rows_loaded[u], 32 * (b - u) + 64)
                need(pe, exp_done, PAIRS * b + p)
                for e in range(2):
                    for t in range(2):
                        last = mm(score_t[:, 512 * e + S * t:512 * e + S * t + S], k_cols(u, p, e, t, P),
                                  q_cols(u, p, 0, S), start=True, stop=True)
                last.then_inc(st_ready, 1)

            def values(b, u, k):
                if k == 0:
                    pe.wait_ge(v_loaded[u], 16 * (b - u) + 32)
                need(pe, o_evac, QUADS * b + k - 1)
                pe.wait_ge(exp_done, PAIRS * b + 2 * k + 2)
                out = pv[(QUADS * u + k) % 2]
                for kind in range(3):
                    tile = min(kind, 1)
                    for t in range(4):
                        a = (t % 2) * 2 * S + tile * S
                        at = S if kind == 2 else 0
                        last = mm(out[32 * t:32 * t + 32, at:at + S], values_of(u, kind, 4 * k + t),
                                  probs[:, slot(u, 2 * k + t // 2), a:a + S],
                                  start=kind != 1, stop=kind != 0)
                last.then_inc(pv_ready, 1)

            def project_out(b, u, m):
                if m == 0:
                    pe.wait_ge(o_ready, b + 1)
                    need(pe, out_done, XC * b)
                elif m == 1:
                    pe.wait_ge(rows_done, min(b + 3, B) if isinstance(b, int) else b + 3)
                else:
                    need(pe, out_done, XC * b + 1)
                r = MT_ROWS[m]
                for k in range(QUADS):
                    last = mm(pj[m % 2][0:r, 0:S], wo_sb[:, k, m * P:m * P + r], o_norm[:, k, :],
                              start=k == 0, stop=k == QUADS - 1)
                last.then_inc(out_ready, 1)

            def maxima_to_rows(b, u):
                pe.wait_ge(max_done, PAIRS * (b + 1))
                need(pe, out_done, XC * (b - 3) + 2)
                for t in range(2):
                    last = nc.tensor.transpose(pj[1][:, t * P:t * P + P], neg_max[:, u, t, :],
                                               ident_sb[:, :])
                last.then_inc(tp_ready, 1)

            pe.wait_ge(ld["small"], 48)
            pe.wait_ge(v_evac, 4 * GROUPS)
            for p in range(PAIRS):
                query_scores(0, 0, p)
            maxima_to_rows(0, 0)

            def batch(b, u):
                final = isinstance(b, int) and b == B - 1
                for what, a in SCHEDULE:
                    if what == "key":
                        key_scores(b, u, a)
                    elif what == "max" and not final:
                        query_scores(b + 1, 1 - u, a)
                    elif what == "tp" and not final:
                        maxima_to_rows(b + 1, 1 - u)
                    elif what == "pv":
                        values(b, u, a)
                    elif what == "out" and not (isinstance(b, int) and b < 2):
                        project_out(b - 2, u, a)

            batches(pe, batch)
            for b in (B - 2, B - 1):
                for m in range(XC):
                    project_out(b, b % 2, m)


TP_STEP = 8
RECIP_STEPS = [0, 2, 4, 6]
SCHEDULE = [
    ("key", 0), ("max", 0),
    ("key", 1), ("max", 1), ("max", 2),
    ("key", 2), ("max", 3), ("out", 0), ("pv", 0),
    ("key", 3), ("out", 1), ("max", 4), ("out", 2), ("max", 5),
    ("key", 4), ("max", 6), ("pv", 1),
    ("key", 5), ("max", 7),
    ("key", 6), ("max", 8), ("pv", 2),
    ("key", 7), ("max", 9),
    ("key", 8), ("tp", 0), ("pv", 3),
    ("key", 9), ("pv", 4),
]

_INS = ["xT", "ctxT", "ctx_sp", "bbox", "wq", "wk", "wv", "wk_ip", "wv_ip", "wo", "bias",
        "grid", "ident", "kaux", "vones"]


def kernel(x, ctx_2048, fside_Bx4x4_0, L0_xattn_w_q, L0_xattn_w_k, L0_xattn_w_v, L0_xattn_w_k_ip,
           L0_xattn_w_v_ip, L0_xattn_w_out, L0_xattn_b_out):
    import numpy as _np
    import concourse.bacc as _bacc
    from concourse import mybir as _mybir
    from concourse.bass_utils import run_bass_kernel_spmd as _run

    f = _np.float32
    ctx = _np.asarray(ctx_2048)
    wo = _np.zeros((QUADS, 4, 32, D), f)
    wo[:, :, :DH] = _np.asarray(L0_xattn_w_out).reshape(QUADS, 4, DH, D)
    bias = _np.zeros((XC * P,), f)
    bias[:D] = _np.asarray(L0_xattn_b_out)
    line = _np.arange(GRID, dtype=f) * f(1.0 / (GRID - 1))
    line[-1] = 1
    gy, gx = _np.meshgrid(line, line, indexing="ij")
    kaux = _np.zeros((32, 2, KEYS), f)
    for e in range(2):
        kaux[e, e, :TEXT] = 1
        kaux[2 + e, e, TEXT:] = 1
    kaux[4, :, TEXT:TEXT + NIP] = 1
    for j in range(NIP):
        kaux[5 + j, :, TEXT + NIP + j] = 1
    vones = _np.ones((P, 1), f)
    vones[P - NSP:] = 0
    arrays = {
        "xT": _np.asarray(x).reshape(B * S, D).T,
        "ctxT": ctx.reshape(B * KEYS, C).T,
        "ctx_sp": ctx[:, TEXT:].reshape(B * NSP, C).T,
        "bbox": _np.asarray(fside_Bx4x4_0).reshape(B, 16),
        "wq": _np.asarray(L0_xattn_w_q), "wk": _np.asarray(L0_xattn_w_k),
        "wv": _np.asarray(L0_xattn_w_v), "wk_ip": _np.asarray(L0_xattn_w_k_ip),
        "wv_ip": _np.asarray(L0_xattn_w_v_ip), "wo": wo.reshape(QUADS * P, D),
        "bias": bias.reshape(XC, P).T,
        "grid": _np.broadcast_to(_np.stack([gx.reshape(-1), gy.reshape(-1)])[None], (B, 2, S)),
        "ident": _np.eye(P, dtype=f), "kaux": kaux.reshape(32, 2 * KEYS), "vones": vones,
    }
    arrays = {n: _np.ascontiguousarray(a) for n, a in arrays.items()}
    nc = _bacc.Bacc("TRN2", target_bir_lowering=False, num_devices=1)
    args = [nc.dram_tensor("in_" + n, arrays[n].shape, _mybir.dt.from_np(arrays[n].dtype),
                           kind="ExternalInput").ap() for n in _INS]
    args.append(nc.dram_tensor("outT", (D, B * S), _mybir.dt.float32, kind="ExternalOutput").ap())
    xattn(nc, *args)
    r = _run(nc, [{"in_" + n: arrays[n] for n in _INS}], core_ids=[0])
    return r.results[0]["outT"].T.reshape(B, S, D)
```

```python
import numpy as np
import concourse.bass as bass
from concourse import mybir
from contextlib import ExitStack

B, S, D, C = 16, 256, 320, 512
H, DH = 20, 16
NIP = 4
KEYS = 256
TEXT = KEYS - 2 * NIP
NSP = KEYS - TEXT
GRID = 16
NEG = -10000.0
PAIRS = H // 2
GB = 2
GROUPS = B // GB
GT = GB * S
QUADS = H // 4
OC = -(-H // 8)
SCALE = DH ** -0.5
P = 128
XC, CC = 3, C // P
MT_ROWS = [128, 128, 64]
VW = 2 * D
AUX = 9
HALF = PAIRS // 2


def xattn(nc, xT, ctxT, ctx_sp, bbox, wq, wk, wv, wk_ip, wv_ip, wo, bias, grid, kaux, vones, outT):
    f32, f32r = mybir.dt.float32, mybir.dt.float32r
    ALU = mybir.AluOpType
    ACT = mybir.ActivationFunctionType
    AX = mybir.AxisListType

    q_parts = nc.dram_tensor("q_parts", [2, D, B * S], f32, kind="Internal").ap()
    k_parts = nc.dram_tensor("k_parts", [2, D, B * KEYS], f32, kind="Internal").ap()
    v_rows = nc.dram_tensor("v_rows", [B, 2, P, VW], f32, kind="Internal").ap()
    v_sp_rows = nc.dram_tensor("v_sp_rows", [B, NSP, VW], f32, kind="Internal").ap()
    aux_rows = nc.dram_tensor("aux_rows", [B, 32, S], f32, kind="Internal").ap()

    ctx = ExitStack()
    with ctx:
        def sb(name, shape, dt=f32):
            return ctx.enter_context(nc.sbuf_tensor(name, shape, dt))

        def sem(name):
            return ctx.enter_context(nc.semaphore(name))

        q_stack = sb("q_stack", [P, 2, PAIRS * S], f32r)
        k_stack = sb("k_stack", [P, 2, PAIRS * 2 * KEYS], f32r)
        probs = sb("probs", [P, 4, 4 * S])
        o_all = sb("o_all", [P, 4 * QUADS * S])
        o_turned = sb("o_turned", [P, QUADS * 2 * S])
        inv_cols = sb("inv_cols", [P, QUADS, 2 * S // 32])
        gate = sb("gate", [32, 2])
        v_cur = sb("v_cur", [P, 2, 3, VW])
        x_res = sb("x_res", [P, 2, XC, S])
        out_sb = sb("out_sb", [P, XC, S])
        wo_sb = sb("wo_sb", [P, OC, D])
        bias_sb = sb("bias_sb", [P, XC])
        max_cols = sb("max_cols", [P, 2, PAIRS, 32], f32r)
        mask_cols = sb("mask_cols", [P, B, 2, AUX - 4])

        x_hi = sb("x_hi", [P, XC, GT], f32r)
        x_lo = sb("x_lo", [P, 2, GT], f32r)
        wq_hi = sb("wq_hi", [P, XC, D], f32r)
        wq_lo = sb("wq_lo", [P, XC, D], f32r)
        wk_hl = sb("wk_hl", [P, 2, CC, D], f32r)
        wv_hl = sb("wv_hl", [P, 2, CC, D], f32r)
        qk_out = sb("qk_out", [P, 2, 2, GT], f32r)
        v_out = sb("v_out", [P, 2, VW])
        vsp_out = sb("vsp_out", [P, VW])
        text_mask = sb("text_mask", [P, 1])
        sp_ctx_hl = sb("sp_ctx_hl", [P, 2, CC, P], f32r)
        boxes = sb("boxes", [B, 16])
        zeros = sb("zeros", [B, S], f32r)
        flat_q = q_stack[:, :, :].rearrange("p a n -> p (a n)")
        c_hi = flat_q[:, 0:CC * GT].rearrange("p (c n) -> p c n", c=CC)
        c_lo = flat_q[:, CC * GT:2 * CC * GT].rearrange("p (c n) -> p c n", c=CC)
        wkip_hl = k_stack[:, 1, 0:2 * CC * D].rearrange("p (s c n) -> p s c n", s=2, c=CC)
        wvip_hl = k_stack[:, 1, 2 * CC * D:4 * CC * D].rearrange("p (s c n) -> p s c n", s=2, c=CC)
        flat_o = o_all
        o_raw = o_all[:, 0:2 * QUADS * S].rearrange("p (k n) -> p k n", k=QUADS)
        at = 2 * QUADS * S
        o_norm = o_all[:, at:at + 2 * OC * S].rearrange("p (u c n) -> p u c n", u=2, c=OC)
        o_norm_t = o_all[:, at + 2 * OC * S:at + 3 * OC * S].rearrange("p (c j n) -> p c j n", c=OC, n=32)
        x_raw = flat_o[:, 0:XC * GT].rearrange("p (c n) -> p c n", c=XC)
        c_raw = flat_o[:, XC * GT:(XC + CC) * GT].rearrange("p (c n) -> p c n", c=CC)
        wq_raw = flat_o[:, (XC + CC) * GT:(XC + CC) * GT + XC * D].rearrange("p (c n) -> p c n", c=XC)
        flat_p = probs[:, :, :].rearrange("p a n -> p (a n)")
        wkip_raw, wvip_raw, wk_raw = (
            flat_p[:, i * CC * D:(i + 1) * CC * D].rearrange("p (c n) -> p c n", c=CC) for i in range(3))
        wv_raw = o_turned[:, 0:CC * D].rearrange("p (c n) -> p c n", c=CC)
        sp_raw = o_turned[:, CC * D:CC * D + CC * P].rearrange("p (c n) -> p c n", c=CC)
        aux_t = flat_p[0:32, 0:B * S]
        aux_q = o_turned[:, 0:B * 2 * 32].rearrange("p (b t n) -> p b t n", b=B, t=2)
        row_buf = v_out[0:32, :, :].rearrange("p a n -> p (a n)")
        kaux_raw = o_turned[96:128, CC * (D + P):CC * (D + P) + 2 * KEYS]
        grid_sb = x_res[0:B, 0, 0:2, :]
        inside = x_res[0:B, 1, :, :]
        covered = x_res[0:B, 0, 2, :]
        mask_out = v_cur[0:B, 0, 0:2, :].rearrange("p k n -> p (k n)").rearrange(
            "p (j n) -> p j n", j=1 + NIP)

        def bank(name, n):
            return ctx.enter_context(nc.psum_tensor(name, [P, n * 512], f32))

        score_t = bank("score_t", 2)
        score_q = bank("score_q", 2)
        pv = [bank("pv0", 1), bank("pv1", 1)]
        pj = [bank("pj0", 1), bank("pj1", 1)]

        ksp_out = [score_t[:, 0:P], score_t[:, 512:512 + P], pv[0][:, 0:P]]

        ld = {n: sem("loaded_" + n) for n in ("sp", "wkip", "wvip", "wq", "wk", "wv", "small", "boxes")}
        w_high = sem("w_high")
        w_low = sem("w_low")
        x_loaded, c_loaded = sem("x_loaded"), sem("c_loaded")
        x_high, c_high = sem("x_high"), sem("c_high")
        x_split, c_split = sem("x_split"), sem("c_split")
        x_tail = sem("x_tail")
        tile_ready = sem("tile_ready")
        hi_done, lo_done = sem("hi_done"), sem("lo_done")
        v_evac = sem("v_evac")
        qk_stored = [sem("qk_stored0"), sem("qk_stored1")]
        v_stored = [sem("v_stored0"), sem("v_stored1")]
        ksp_ready, ksp_hi, ksp_lo = sem("ksp_ready"), sem("ksp_hi"), sem("ksp_lo")
        ksp_stored = [sem("ksp_stored0"), sem("ksp_stored1")]
        vsp_ready, vsp_done = sem("vsp_ready"), sem("vsp_done")
        sp_stored = sem("sp_stored")
        preset, mask_step, mask_done = sem("preset"), sem("mask_step"), sem("mask_done")
        kaux_step = sem("kaux_step")
        aux_stored = sem("aux_stored")
        stacks_set = sem("stacks_set")
        stack_loaded = [[sem(f"stack_loaded{a}{h}") for h in range(2)] for a in range(2)]
        v_loaded = [sem("v_loaded0"), sem("v_loaded1")]
        xr_loaded = [sem("xr_loaded0"), sem("xr_loaded1")]
        sq_ready, max_done = sem("sq_ready"), sem("max_done")
        mask_cols_step = sem("mask_cols_step")
        mask_put = sem("mask_put")
        rows_turned = sem("rows_turned")
        rows_loaded = [sem("rows_loaded0"), sem("rows_loaded1")]
        aux_t_loaded = sem("aux_t_loaded")
        st_ready, exp_done = sem("st_ready"), sem("exp_done")
        pv_ready, o_evac = sem("pv_ready"), sem("o_evac")
        turned, inv_done, scaled = sem("turned"), sem("inv_done"), sem("scaled")
        o_added = sem("o_added")
        o_ready = sem("o_ready")
        out_ready, out_done, out_stored = sem("out_ready"), sem("out_done"), sem("out_stored")

        def need(eng, s, value):
            if not isinstance(value, int) or value > 0:
                eng.wait_ge(s, value)

        def values_of(par, kind, h):
            return v_cur[:, par, kind, 2 * DH * h:2 * DH * (h + 1)]

        def halves(row):
            r = row.rearrange("p (h s n) -> p h s n", h=H, s=2)
            return r[:, :, 0, :], r[:, :, 1, :]

        def by_head(row):
            return row.rearrange("p (h n) -> p h n", h=H)

        def q_cols(par, p, a, n):
            return q_stack[:, par, p * S + a:p * S + a + n]

        def k_cols(par, p, head, tile, n):
            at = (2 * p + head) * KEYS + tile * P
            return k_stack[:, par, at:at + n]

        def turned_blocks(k):
            return o_turned[:, k * 2 * S:(k + 1) * 2 * S].rearrange("p (j n) -> p j n", n=32)

        slot = lambda u, p: (PAIRS * u + p) % 4

        def there(b, off=0):
            return not isinstance(b, int) or 0 <= b + off < B

        def batches(eng, body, tail=True):
            for u in range(2):
                body(u, u)
            with eng.Fori(1, B // 2 - 1) as i:
                for u in range(2):
                    body(2 * i + u, u)
            for b in (B - 2, B - 1):
                body(b, b % 2)
            if tail:
                body(B, 0)

        def groups(eng, body):
            body(0)
            with eng.Fori(1, GROUPS) as g:
                body(g)

        block = ctx.enter_context(nc.Block())

        @block.sync
        def _(sp):
            def rows(a):
                return a.rearrange("(c p) n -> p c n", p=P)

            def load_wq():
                sp.dma_start(wq_raw[:, 0:2, :], rows(wq[0:256, :])).then_inc(ld["wq"], 16)
                for at in (0, 64):
                    sp.dma_start(wq_raw[at:at + 64, 2, :], wq[256:320, :]).then_inc(ld["wq"], 16)

            sp.dma_start(sp_raw, rows(ctx_sp)).then_inc(ld["sp"], 16)
            sp.dma_start(wkip_raw, rows(wk_ip)).then_inc(ld["wkip"], 16)
            sp.dma_start(wvip_raw, rows(wv_ip)).then_inc(ld["wvip"], 16)
            load_wq()

            def load_group(g):
                need(sp, x_tail, g)
                cols = bass.ds(g * GT, GT)
                sp.dma_start(x_raw[:, 0:2, :], rows(xT[0:256, cols])).then_inc(x_loaded, 16)
                for at in (0, 64):
                    sp.dma_start(x_raw[at:at + 64, 2, :], xT[256:320, cols]).then_inc(x_loaded, 16)
                need(sp, c_split, g)
                sp.dma_start(c_raw, rows(ctxT[:, cols])).then_inc(c_loaded, 16)

            def store_group(g):
                for j in range(6):
                    m, r = j % 3, MT_ROWS[j % 3]
                    src = qk_out[0:r, j % 2, :, :].bitcast(f32)
                    sp.wait_ge(lo_done, 6 * g + j + 1)
                    for s in range(2):
                        if j < 3:
                            sp.dma_start(q_parts[s, m * P:m * P + r, bass.ds(g * GT, GT)], src[:, s, :])\
                                .then_inc(qk_stored[j % 2], 16)
                        else:
                            dst = k_parts[s].rearrange("p (b n) -> p b n", n=KEYS)[
                                m * P:m * P + r, bass.ds(g * GB, GB), 0:TEXT]
                            sp.dma_start(dst, src[:, s].rearrange("p (b n) -> p b n", b=GB)[:, :, 0:TEXT])\
                                .then_inc(qk_stored[j % 2], 16)
                for t in range(2 * GB):
                    sp.wait_ge(v_evac, 4 * g + t + 1)
                    dst = v_rows.rearrange("b k p n -> (b k) p n")[bass.ds(2 * GB * g + t, 1), :, :]
                    sp.dma_start(dst.rearrange("a p n -> (a p) n"), v_out[:, t % 2, :])\
                        .then_inc(v_stored[t % 2], 16)

            load_group(0)
            sp.dma_start(wk_raw, rows(wk)).then_inc(ld["wk"], 16)
            sp.dma_start(wv_raw, rows(wv)).then_inc(ld["wv"], 16)
            sp.dma_start(wo_sb[:, :, :], rows(wo)).then_inc(ld["small"], 16)
            sp.dma_start(bias_sb[:, :], bias).then_inc(ld["small"], 16)
            with sp.Fori(1, GROUPS) as g:
                load_group(g)
                store_group(g - 1)
            sp.wait_ge(aux_stored, 48)
            sp.dma_start(aux_t.rearrange("r (b n) -> r b n", b=B), aux_rows.rearrange("b r n -> r b n"))\
                .then_inc(aux_t_loaded, 16)
            store_group(GROUPS - 1)

            def load_stack(b, u, h):
                ps, n = h * HALF, HALF
                done = stack_loaded[u][h]
                cols = bass.ds(b * S, S)
                qv = q_stack[:, u, ps * S:(ps + n) * S].rearrange("p (a n) -> p a n", a=n).bitcast(f32)
                kv = k_stack[:, u, ps * 2 * KEYS:(ps + n) * 2 * KEYS].rearrange(
                    "p (a e n) -> p a e n", a=n, e=2).bitcast(f32)
                for quad, part in enumerate((0, 1, 0)):
                    src = q_parts[part, 32 * ps:32 * (ps + n), cols].rearrange("(a r) n -> r a n", r=32)
                    sp.dma_start(qv[32 * quad:32 * quad + 32, :, :], src).then_inc(done, 16)
                for quad, part in enumerate((0, 0, 1)):
                    src = k_parts[part, 32 * ps:32 * (ps + n), cols].rearrange(
                        "(a e r) n -> e r a n", e=2, r=DH)
                    for e in range(2):
                        at = 32 * quad + DH * e
                        sp.dma_start(kv[at:at + DH, :, e, :], src[e]).then_inc(done, 16)
                src = aux_rows[bass.ds(b, 1), :, :].rearrange("a r n -> (a r) n")
                sp.dma_start(qv[96:128, :, :], src.unsqueeze(1).broadcast_to([32, n, S])).then_inc(done, 16)

            def load_values(b, u):
                sp.dma_start(v_cur[:, u, 0:2, :], v_rows[bass.ds(b, 1), :, :, :].rearrange(
                    "a k p n -> (a p) k n")).then_inc(v_loaded[u], 16)
                sp.dma_start(v_cur[P - NSP:P, u, 2, :], v_sp_rows[bass.ds(b, 1), :, :].rearrange(
                    "a p n -> (a p) n")).then_inc(v_loaded[u], 16)

            def load_residual(b, u):
                cols = bass.ds(b * S, S)
                sp.dma_start(x_res[:, u, 0:2, :], rows(xT[0:256, cols])).then_inc(xr_loaded[u], 16)
                sp.dma_start(x_res[0:64, u, 2, :], xT[256:320, cols]).then_inc(xr_loaded[u], 16)

            for s in (0, 1):
                sp.wait_ge(qk_stored[s], 32 * 3 * GROUPS)
                sp.wait_ge(v_stored[s], 16 * 2 * GROUPS)
                sp.wait_ge(ksp_stored[s], 32 * (2 - s))
            sp.wait_ge(sp_stored, 16)
            sp.wait_ge(stacks_set, 2)
            sp.wait_ge(tile_ready, 10 * GROUPS)
            sp.wait_ge(mask_done, 1)
            load_stack(0, 0, 0)
            load_stack(0, 0, 1)
            load_values(0, 0)
            load_stack(1, 1, 0)

            def load_rows(b, u, h):
                sp.wait_ge(rows_turned, 2 * b + h + 1)
                sp.dma_start(q_stack[96:128, u, h * HALF * S:(h + 1) * HALF * S].bitcast(f32), row_buf)\
                    .then_inc(rows_loaded[h], 16)

            load_rows(0, 0, 0)

            def batch(b, u):
                load_rows(b, u, 1)
                if there(b, 1):
                    need(sp, st_ready, 2 * PAIRS * b)
                    load_stack(b + 1, 1 - u, 1)
                if there(b, -2):
                    store_out(b - 2)
                load_residual(b, u)
                if there(b, 1):
                    need(sp, pv_ready, QUADS * b)
                    load_values(b + 1, 1 - u)
                    load_rows(b + 1, 1 - u, 0)
                if there(b, 2):
                    sp.wait_ge(st_ready, 2 * PAIRS * b + PAIRS)
                    load_stack(b + 2, u, 0)

            def store_out(b):
                need(sp, out_done, XC * (b + 1))
                cols = bass.ds(b * S, S)
                sp.dma_start(rows(outT[0:256, cols]), out_sb[:, 0:2, :]).then_inc(out_stored, 16)
                sp.dma_start(outT[256:320, cols], out_sb[0:64, 2, :]).then_inc(out_stored, 16)

            batches(sp, batch, tail=False)
            for b in (B - 2, B - 1):
                store_out(b)
            sp.wait_ge(out_stored, 32 * B)

        @block.gpsimd
        def _(pool):
            pool.dma_start(boxes[:, :], bbox).then_inc(ld["boxes"], 16)
            pool.dma_start(grid_sb, grid).then_inc(ld["boxes"], 16)
            pool.dma_start(kaux_raw, kaux).then_inc(ld["boxes"], 16)
            pool.dma_start(text_mask[:, :], vones).then_inc(ld["boxes"], 16)
            pool.memset(zeros[:, :].bitcast(f32), 0.0).then_inc(preset, 1)
            pool.memset(v_cur[:, :, 2, :], 0.0).then_inc(preset, 1)
            pool.memset(halves(v_out[:, 0, :])[1], 1.0).then_inc(preset, 1)
            pool.memset(halves(vsp_out[:, :])[1], 1.0).then_inc(preset, 1)
            pool.memset(halves(v_out[:, 1, :])[1], 1.0).then_inc(preset, 1)
            pool.memset(max_cols[:, :, :, :].bitcast(f32), 0.0).then_inc(preset, 1)
            pool.memset(k_stack[0:96, 0, :].bitcast(f32), 0.0).then_inc(kaux_step, 1)
            pool.wait_ge(ld["boxes"], 64)
            pool.wait_ge(preset, 6)
            pool.tensor_scalar(halves(v_out[:, 1, :])[1], halves(v_out[:, 1, :])[1], text_mask[:, 0:1], None,
                               ALU.mult).then_inc(preset, 1)
            pool.dma_start(aux_rows[:, 0:4, :], zeros[:, :].bitcast(f32).unsqueeze(1).broadcast_to([B, 4, S])).then_inc(aux_stored, 16)
            pool.dma_start(aux_rows[:, AUX:32, :], zeros[:, :].bitcast(f32).unsqueeze(1).broadcast_to([B, 32 - AUX, S])).then_inc(aux_stored, 16)

            def constant_rows(u):
                pool.tensor_copy(
                    k_stack[96:128, u, :].rearrange("p (a n) -> p a n", a=PAIRS),
                    kaux_raw.unsqueeze(1).broadcast_to([32, PAIRS, 2 * KEYS])).then_inc(stacks_set, 1)

            for m, r in enumerate(MT_ROWS):
                pool.wait_ge(ksp_lo, m + 1)
                src = qk_out[0:r, m % 2, :, 0:P].rearrange("p s (b n) -> p s b n", b=B).bitcast(f32)
                dst = k_parts[:, m * P:m * P + r, :].rearrange("s p (b n) -> s p b n", b=B)
                for s in range(2):
                    pool.dma_start(dst[s, :, :, TEXT:KEYS], src[:, s]).then_inc(ksp_stored[m % 2], 16)
            pool.wait_ge(vsp_done, 1)
            pool.dma_start(v_sp_rows.rearrange("b p n -> (b p) n"), vsp_out[:, :]).then_inc(sp_stored, 16)

            pool.wait_ge(w_low, 4)
            pool.memset(o_norm_t[:, :, :, :], 0.0).then_inc(preset, 1)

            pool.wait_ge(preset, 8)
            pool.wait_ge(kaux_step, 1)
            constant_rows(0)
            pool.wait_ge(vsp_ready, 1)
            pool.wait_ge(stacks_set, 1)
            pool.memset(k_stack[0:96, 1, :].bitcast(f32), 0.0).then_inc(kaux_step, 1)
            pool.wait_ge(kaux_step, 2)
            constant_rows(1)
            pool.wait_ge(mask_done, 1)
            pool.dma_start(aux_rows[:, 4:AUX, :], mask_out).then_inc(aux_stored, 16)

            def normalise(b, u):
                for k in range(QUADS):
                    n = QUADS * b + k
                    out = turned_blocks(k)[:, :, 0:DH]
                    pool.wait_ge(inv_done, n + 1)
                    pool.tensor_tensor(out, out, inv_cols[:, k, :].unsqueeze(2).broadcast_to(
                        [P, 2 * S // 32, DH]), ALU.mult).then_inc(scaled, 1)
                    pool.wait_ge(scaled, n + 1)
                    need(pool, o_ready, OC * (b - 1) + k // 2 + 1)
                    half = (k % 2) * DH
                    pool.tensor_tensor(o_norm_t[:, k // 2, :, half:half + DH], out[:, 0:S // 32, :],
                                       out[:, S // 32:, :], ALU.add).then_inc(o_added, 1)

            batches(pool, normalise, tail=False)

        @block.scalar
        def _(act):
            def high(dst, src, loaded, value):
                act.wait_ge(loaded, value)
                nc.scalar.activation(dst, src, ACT.Copy).then_inc(w_high, 1)

            high(sp_ctx_hl[:, 0], sp_raw, ld["sp"], 16)
            high(wkip_hl[:, 0], wkip_raw, ld["wkip"], 16)
            high(wvip_hl[:, 0], wvip_raw, ld["wvip"], 16)
            high(wq_hi[:, :, :], wq_raw, ld["wq"], 48)

            def group(g):
                act.wait_ge(x_loaded, 48 * (g + 1))
                need(act, tile_ready, 10 * (g - 1) + 3)
                nc.scalar.activation(x_hi[:, :, :], x_raw, ACT.Copy).then_inc(x_high, 1)
                act.wait_ge(c_loaded, 16 * (g + 1))
                need(act, tile_ready, 10 * g)
                nc.scalar.activation(c_hi, c_raw, ACT.Copy).then_inc(c_high, 1)
                if isinstance(g, int) and g == 0:
                    high(wk_hl[:, 0], wk_raw, ld["wk"], 16)
                    high(wv_hl[:, 0], wv_raw, ld["wv"], 16)
                    act.wait_ge(ksp_stored[0], 64)
                    act.wait_ge(ksp_stored[1], 32)
                for j in range(6):
                    r = MT_ROWS[j % 3]
                    act.wait_ge(tile_ready, 10 * g + j + 1)
                    need(act, qk_stored[j % 2], 32 * (3 * g + j // 2))
                    nc.scalar.activation(qk_out[0:r, j % 2, 0, :], pj[j % 2][0:r, :], ACT.Copy)\
                        .then_inc(hi_done, 1)
                for t in range(4):
                    act.wait_ge(tile_ready, 10 * g + 7 + t)
                    need(act, v_stored[t % 2], 16 * (2 * g + t // 2))
                    if t % 2:
                        nc.scalar.activation(halves(v_out[:, 1, :])[0], by_head(pj[1][:, 0:D]), ACT.Copy,
                                             scale=text_mask[:, 0:1]).then_inc(v_evac, 1)
                    else:
                        nc.scalar.activation(halves(v_out[:, 0, :])[0], by_head(pj[0][:, 0:D]), ACT.Copy).then_inc(v_evac, 1)

            for m, r in enumerate(MT_ROWS):
                act.wait_ge(ksp_ready, m + 1)
                if m == 2:
                    act.wait_ge(ksp_stored[0], 32)
                nc.scalar.activation(qk_out[0:r, m % 2, 0, 0:P], ksp_out[m][0:r, :], ACT.Copy)\
                    .then_inc(ksp_hi, 1)
            act.wait_ge(vsp_ready, 1)
            nc.scalar.activation(halves(vsp_out[:, :])[0], by_head(score_q[:, 0:D]), ACT.Copy).then_inc(vsp_done, 1)
            act.wait_ge(preset, 7)
            groups(act, group)

            def evacuate(b, u, k):
                n = QUADS * b + k
                act.wait_ge(pv_ready, n + 1)
                need(act, turned, n + 1 - QUADS)
                nc.scalar.activation(o_raw[:, k, :], pv[(QUADS * u + k) % 2][:, :], ACT.Copy)\
                    .then_inc(o_evac, 1)

            def batch(b, u):
                for p in range(PAIRS):
                    for e in range(2):
                        if there(b):
                            act.wait_ge(st_ready, 2 * (PAIRS * b + p) + e + 1)
                            if p % 2 == 0 and e == 0:
                                need(act, pv_ready, QUADS * b + (p - 4) // 2 + 1)
                            nc.scalar.activation(probs[:, slot(u, p), 2 * S * e:2 * S * (e + 1)],
                                                 score_t[:, 512 * e:512 * e + 512], ACT.Exp, scale=SCALE)\
                                .then_inc(exp_done, 1)
                        if e == 0:
                            for k, off in EVACUATE.get(p, ()):
                                if there(b, off):
                                    evacuate(b + off, (u + off) % 2, k)

            batches(act, batch)

        @block.vector
        def _(dve):
            steps = [0]

            def then(ins):
                steps[0] += 1
                ins.then_inc(mask_step, 1)
                dve.wait_ge(mask_step, steps[0])

            def mask():
                dve.wait_ge(ld["boxes"], 64)
                gx, gy = grid_sb[:, 0, :], grid_sb[:, 1, :]
                for j in range(NIP):
                    side = lambda c: boxes[:, 4 * j + c:4 * j + c + 1]
                    at = inside_j(j)
                    then(nc.vector.tensor_scalar(at, gx, side(0), None, ALU.is_ge))
                    for g, c, op in ((gx, 2, ALU.is_le), (gy, 1, ALU.is_ge), (gy, 3, ALU.is_le)):
                        then(nc.vector.scalar_tensor_tensor(out=at, in0=g, scalar=side(c), in1=at,
                                                            op0=op, op1=ALU.mult))
                    then(nc.vector.tensor_scalar(mask_out[:, 1 + j, :], at, -NEG / SCALE, NEG / SCALE,
                                                 ALU.mult, ALU.add))
                    if j == 0:
                        then(nc.vector.tensor_copy(covered, at))
                    else:
                        then(nc.vector.tensor_tensor(covered, covered, at, ALU.max))
                nc.vector.tensor_scalar(mask_out[:, 0, :], covered, NEG / SCALE, None, ALU.mult)\
                    .then_inc(mask_done, 1)

            def inside_j(j):
                return inside[:, j % 3, :]

            n_low = [0]

            def low(dst, raw, hi):
                n_low[0] += 1
                dve.wait_ge(w_high, n_low[0])
                nc.vector.tensor_tensor(dst, raw, hi.bitcast(f32), ALU.subtract).then_inc(w_low, 1)

            low(sp_ctx_hl[:, 1], sp_raw, sp_ctx_hl[:, 0])
            low(wkip_hl[:, 1], wkip_raw, wkip_hl[:, 0])
            low(wvip_hl[:, 1], wvip_raw, wvip_hl[:, 0])
            low(wq_lo[:, :, :], wq_raw, wq_hi[:, :, :])

            for m, r in enumerate(MT_ROWS):
                dve.wait_ge(ksp_hi, m + 1)
                if m == 2:
                    dve.wait_ge(ksp_stored[0], 32)
                nc.vector.tensor_tensor(qk_out[0:r, m % 2, 1, 0:P], ksp_out[m][0:r, :],
                                        qk_out[0:r, m % 2, 0, 0:P].bitcast(f32), ALU.subtract)\
                    .then_inc(ksp_lo, 1)

            def group(g):
                dve.wait_ge(x_high, g + 1)
                nc.vector.tensor_tensor(x_lo[:, :, :], x_raw[:, 0:2, :], x_hi[:, 0:2, :].bitcast(f32),
                                        ALU.subtract).then_inc(x_split, 1)
                nc.vector.tensor_tensor(x_hi[64:128, 2, :], x_raw[64:128, 2, :],
                                        x_hi[64:128, 2, :].bitcast(f32), ALU.subtract).then_inc(x_tail, 1)
                dve.wait_ge(c_high, g + 1)
                nc.vector.tensor_tensor(c_lo, c_raw, c_hi.bitcast(f32), ALU.subtract).then_inc(c_split, 1)
                if isinstance(g, int) and g == 0:
                    low(wk_hl[:, 1], wk_raw, wk_hl[:, 0])
                    low(wv_hl[:, 1], wv_raw, wv_hl[:, 0])
                for j in range(6):
                    r = MT_ROWS[j % 3]
                    dve.wait_ge(hi_done, 6 * g + j + 1)
                    nc.vector.tensor_tensor(qk_out[0:r, j % 2, 1, :], pj[j % 2][0:r, :],
                                            qk_out[0:r, j % 2, 0, :].bitcast(f32), ALU.subtract)\
                        .then_inc(lo_done, 1)
                if isinstance(g, int) and g == 0:
                    mask()

            groups(dve, group)

            def put_mask(b, h):
                need(dve, rows_turned, 2 * b + h - 1)
                nc.vector.memset(gate[:, h:h + 1], 0.0)
                to = max_cols[:, :, h * HALF:(h + 1) * HALF, 4:AUX]
                what = mask_cols[:, bass.ds(b, 1), :, :].rearrange("p b t n -> p (b t) n")
                nc.vector.tensor_copy(to, what.unsqueeze(2).broadcast_to([P, 2, HALF, AUX - 4]))\
                    .then_inc(mask_put, 1)

            def maxima(b, p, t):
                if p % HALF == 0 and t == 0:
                    put_mask(b, p // HALF)
                dve.wait_ge(sq_ready, 2 * (PAIRS * b + p) + t + 1)
                both = score_q[:, 512 * t:512 * t + 512].rearrange("p (e n) -> p e n", e=2)
                nc.vector.tensor_reduce(out=max_cols[:, t, p, 0:2], in_=both[:, :, 0:TEXT],
                                        op=ALU.max, axis=AX.X, negate=True)
                nc.vector.tensor_reduce(out=max_cols[:, t, p, 2:4], in_=both[:, :, TEXT:KEYS],
                                        op=ALU.max, axis=AX.X, negate=True).then_inc(max_done, 1)

            def turn(b, h):
                dve.wait_ge(max_done, 2 * (PAIRS * b + HALF * (h + 1)))
                dve.wait_ge(mask_put, 2 * b + h + 1)
                need(dve, rows_loaded[1 - h], 16 * (b + h))
                to = row_buf.rearrange("r (a t i n) -> r t a i n", a=HALF, t=2, i=4)
                for i in range(4):
                    last = nc.vector.transpose(
                        to[:, :, :, i, :],
                        max_cols[32 * i:32 * i + 32, :, h * HALF:(h + 1) * HALF, :].bitcast(f32))
                last.then_inc(rows_turned, 1)

            def invert(b, k):
                n = QUADS * b + k
                dve.wait_ge(o_evac, n + 1)
                need(dve, o_added, n + 1 - QUADS)
                nc.vector.transpose(turned_blocks(k), o_raw[:, k, :].rearrange("p (j n) -> p j n", n=32))\
                    .then_inc(turned, 1)
                dve.wait_ge(turned, n + 1)
                nc.vector.reciprocal(inv_cols[:, k, :], turned_blocks(k)[:, :, DH]).then_inc(inv_done, 1)

            def turn_back(b, u, c):
                dve.wait_ge(o_added, QUADS * b + min(2 * c + 2, QUADS))
                if c == 0:
                    need(dve, out_ready, XC * (b - 1))
                nc.vector.transpose(o_norm[:, u, c, :].rearrange("p (j n) -> p j n", n=32),
                                    o_norm_t[:, c, :, :]).then_inc(o_ready, 1)

            dve.wait_ge(aux_t_loaded, 16)
            by_block = aux_t.rearrange("r (b t i n) -> r b t i n", b=B, t=2, i=4)
            for i in range(4):
                last = nc.vector.transpose(aux_q[32 * i:32 * i + 32, :, :, :], by_block[:, :, :, i, :])
            last.then_inc(mask_cols_step, 1)
            dve.wait_ge(mask_cols_step, 1)
            nc.vector.tensor_copy(mask_cols[:, :, :, :], aux_q[:, :, :, 4:AUX]).then_inc(mask_cols_step, 1)
            dve.wait_ge(mask_cols_step, 2)
            dve.wait_ge(preset, 7)

            def finish(b, u, m):
                r = MT_ROWS[m]
                dve.wait_ge(out_ready, XC * b + m + 1)
                if m == 0:
                    need(dve, out_stored, 32 * b)
                    dve.wait_ge(xr_loaded[u], 16 * (b - u) + 32)
                nc.vector.scalar_tensor_tensor(
                    out=out_sb[0:r, m, :], in0=pj[m % 2][0:r, 0:S], scalar=bias_sb[0:r, m:m + 1],
                    in1=x_res[0:r, u, m, :], op0=ALU.add, op1=ALU.add).then_inc(out_done, 1)

            dve.wait_ge(ld["small"], 32)
            for p in range(PAIRS):
                for t in range(2):
                    maxima(0, p, t)
                if p % HALF == HALF - 1:
                    turn(0, p // HALF)

            def batch(b, u):
                for p in range(PAIRS):
                    for t in range(2):
                        if there(b, 1) and there(b):
                            maxima(b + 1, p, t)
                        if t == 0:
                            for k, off in INVERT.get(p, ()):
                                if there(b, off):
                                    invert(b + off, k)
                            for c, off in TURN_BACK.get(p, ()):
                                if there(b, off):
                                    turn_back(b + off, (u + off) % 2, c)
                            for m, off in FINISH.get(p, ()):
                                if there(b, off):
                                    finish(b + off, (u + off) % 2, m)
                    if p % HALF == HALF - 1 and there(b, 1) and there(b):
                        turn(b + 1, p // HALF)

            batches(dve, batch)
        @block.tensor
        def _(pe):
            mm = nc.tensor.matmul

            def three(out, w_hi, w_lo, x_hi_, x_lo_, start, stop):
                mm(out, w_hi, x_hi_, start=start, stop=False)
                mm(out, w_lo, x_hi_, start=False, stop=False)
                return mm(out, w_hi, x_lo_, start=False, stop=stop)

            pe.wait_ge(w_low, 2)
            for m, r in enumerate(MT_ROWS):
                for c in range(CC):
                    last = three(ksp_out[m][0:r, :], wkip_hl[:, 0, c, m * P:m * P + r],
                                 wkip_hl[:, 1, c, m * P:m * P + r], sp_ctx_hl[:, 0, c, :],
                                 sp_ctx_hl[:, 1, c, :], c == 0, c == CC - 1)
                last.then_inc(ksp_ready, 1)
            pe.wait_ge(w_low, 3)
            for c in range(CC):
                last = three(score_q[:, 0:D], sp_ctx_hl[:, 0, c, :], sp_ctx_hl[:, 1, c, :],
                             wvip_hl[:, 0, c, :], wvip_hl[:, 1, c, :], c == 0, c == CC - 1)
            last.then_inc(vsp_ready, 1)

            def group(g):
                first = isinstance(g, int) and g == 0
                if first:
                    pe.wait_ge(w_low, 4)
                pe.wait_ge(x_tail, g + 1)
                for j in range(6):
                    m, r = j % 3, MT_ROWS[j % 3]
                    out = pj[j % 2][0:r, :]
                    cols = slice(m * P, m * P + r)
                    if j < 2:
                        need(pe, v_evac, 4 * g - 1 + j)
                    else:
                        pe.wait_ge(lo_done, 6 * g + j - 1)
                    if j < 3:
                        for c in range(2):
                            three(out, wq_hi[:, c, cols], wq_lo[:, c, cols], x_hi[:, c, :], x_lo[:, c, :],
                                  c == 0, False)
                        mm(out, wq_hi[:, 2, cols], x_hi[:, 2, :], start=False, stop=False)
                        last = mm(out, wq_lo[:, 2, cols], x_hi[:, 2, :], start=False, stop=True)
                    else:
                        if j == 3:
                            pe.wait_ge(c_split, g + 1)
                            if first:
                                pe.wait_ge(w_low, 5)
                        for c in range(CC):
                            last = three(out, wk_hl[:, 0, c, cols], wk_hl[:, 1, c, cols], c_hi[:, c, :],
                                         c_lo[:, c, :], c == 0, c == CC - 1)
                    last.then_inc(tile_ready, 1)
                if first:
                    pe.wait_ge(w_low, 6)
                for t in range(2 * GB):
                    if t < 2:
                        pe.wait_ge(lo_done, 6 * g + 5 + t)
                    else:
                        pe.wait_ge(v_evac, 4 * g + t - 1)
                    keys = slice(t * P, t * P + P)
                    for c in range(CC):
                        last = three(pj[t % 2][:, 0:D], c_hi[:, c, keys], c_lo[:, c, keys],
                                     wv_hl[:, 0, c, :], wv_hl[:, 1, c, :], c == 0, c == CC - 1)
                    last.then_inc(tile_ready, 1)

            groups(pe, group)

            def query_scores(b, u, p, t):
                if p % HALF == 0 and t == 0:
                    pe.wait_ge(stack_loaded[u][p // HALF], 80 * (b - u) + 160)
                need(pe, max_done, 2 * (PAIRS * b + p) + t - 1)
                mm(score_q[:, 512 * t:512 * t + 512], q_cols(u, p, t * P, P),
                   k_cols(u, p, 0, 0, 2 * KEYS), start=True, stop=True).then_inc(sq_ready, 1)

            def key_scores(b, u, p, e):
                if p % HALF == 0 and e == 0:
                    pe.wait_ge(rows_loaded[p // HALF], 16 * (b + 1))
                need(pe, exp_done, 2 * (PAIRS * b + p) + e - 1)
                for t in range(2):
                    last = mm(score_t[:, 512 * e + S * t:512 * e + S * t + S], k_cols(u, p, e, t, P),
                              q_cols(u, p, 0, S), start=True, stop=True)
                last.then_inc(st_ready, 1)

            def values(b, u, k, kinds):
                if k == 0 and 0 in kinds:
                    pe.wait_ge(v_loaded[u], 16 * (b - u) + 32)
                if 0 in kinds:
                    need(pe, o_evac, QUADS * b + k - 1)
                    pe.wait_ge(exp_done, 2 * PAIRS * b + 4 * (k + 1))
                out = pv[(QUADS * u + k) % 2]
                for kind in kinds:
                    tile = min(kind, 1)
                    for t in range(4):
                        a = (t % 2) * 2 * S + tile * S
                        at = S if kind == 2 else 0
                        last = mm(out[32 * t:32 * t + 32, at:at + S], values_of(u, kind, 4 * k + t),
                                  probs[:, slot(u, 2 * k + t // 2), a:a + S],
                                  start=kind != 1, stop=kind != 0)
                if 2 in kinds:
                    last.then_inc(pv_ready, 1)

            def project_out(b, u, m, k):
                if m == 0:
                    pe.wait_ge(o_ready, OC * b + k + 1)
                if k == 0:
                    need(pe, out_done, XC * b + (0, -1, 1)[m])
                r = MT_ROWS[m]
                last = mm(pj[m % 2][0:r, 0:S], wo_sb[:, k, m * P:m * P + r], o_norm[:, u, k, :],
                          start=k == 0, stop=k == OC - 1)
                if k == OC - 1:
                    last.then_inc(out_ready, 1)

            pe.wait_ge(ld["small"], 32)
            pe.wait_ge(v_evac, 4 * GROUPS)
            for p in range(PAIRS):
                for t in range(2):
                    query_scores(0, 0, p, t)

            def batch(b, u):
                for p in range(PAIRS):
                    for half in range(2):
                        if there(b):
                            key_scores(b, u, p, half)
                        if there(b) and there(b, 1):
                            query_scores(b + 1, 1 - u, p, half)
                        if half == 0:
                            for k, kinds, off in VALUES.get(p, ()):
                                if there(b, off):
                                    values(b + off, (u + off) % 2, k, kinds)
                        else:
                            for m, k in OUT.get(p, ()):
                                if there(b, -1):
                                    project_out(b - 1, 1 - u, m, k)

            batches(pe, batch)


VALUES = {p: [((p - 2) // 2, (0,) if p % 2 == 0 else (1, 2), 0)] for p in range(2, PAIRS)}
VALUES[0], VALUES[1] = [(QUADS - 1, (0,), -1)], [(QUADS - 1, (1, 2), -1)]
EVACUATE = {4: [(0, 0)], 6: [(1, 0)], 8: [(2, 0)], 0: [(3, -1)], 2: [(4, -1)]}
INVERT = {5: [(0, 0)], 7: [(1, 0)], 9: [(2, 0)], 1: [(3, -1)], 3: [(4, -1)]}
TURN_BACK = {9: [(0, 0)], 2: [(1, -1)], 4: [(2, -1)]}
OUT = {p: [(i // OC, i % OC) for i in range(2 * (p - 4), min(2 * (p - 4) + 2, XC * OC))]
       for p in range(4, PAIRS)}
FINISH = {6: [(0, -1)], 8: [(1, -1)], 9: [(2, -1)]}

_INS = ["xT", "ctxT", "ctx_sp", "bbox", "wq", "wk", "wv", "wk_ip", "wv_ip", "wo", "bias",
        "grid", "kaux", "vones"]


def kernel(x, ctx_2048, fside_Bx4x4_0, L0_xattn_w_q, L0_xattn_w_k, L0_xattn_w_v, L0_xattn_w_k_ip,
           L0_xattn_w_v_ip, L0_xattn_w_out, L0_xattn_b_out):
    import numpy as _np
    import concourse.bacc as _bacc
    from concourse import mybir as _mybir
    from concourse.bass_utils import run_bass_kernel_spmd as _run

    f = _np.float32
    ctx = _np.asarray(ctx_2048)
    wo = _np.zeros((2 * OC, 4, DH, D), f)
    wo[:QUADS] = _np.asarray(L0_xattn_w_out).reshape(QUADS, 4, DH, D)
    wo = wo.reshape(OC, 2, 4, DH, D).transpose(0, 2, 1, 3, 4)
    bias = _np.zeros((XC * P,), f)
    bias[:D] = _np.asarray(L0_xattn_b_out)
    line = _np.arange(GRID, dtype=f) * f(1.0 / (GRID - 1))
    line[-1] = 1
    gy, gx = _np.meshgrid(line, line, indexing="ij")
    kaux = _np.zeros((32, 2, KEYS), f)
    for e in range(2):
        kaux[e, e, :TEXT] = 1
        kaux[2 + e, e, TEXT:] = 1
    kaux[4, :, TEXT:TEXT + NIP] = 1
    for j in range(NIP):
        kaux[5 + j, :, TEXT + NIP + j] = 1
    vones = _np.ones((P, 1), f)
    vones[P - NSP:] = 0
    arrays = {
        "xT": _np.asarray(x).reshape(B * S, D).T,
        "ctxT": ctx.reshape(B * KEYS, C).T,
        "ctx_sp": ctx[:, TEXT:].reshape(B * NSP, C).T,
        "bbox": _np.asarray(fside_Bx4x4_0).reshape(B, 16),
        "wq": _np.asarray(L0_xattn_w_q), "wk": _np.asarray(L0_xattn_w_k),
        "wv": _np.asarray(L0_xattn_w_v), "wk_ip": _np.asarray(L0_xattn_w_k_ip),
        "wv_ip": _np.asarray(L0_xattn_w_v_ip), "wo": wo.reshape(OC * P, D),
        "bias": bias.reshape(XC, P).T,
        "grid": _np.broadcast_to(_np.stack([gx.reshape(-1), gy.reshape(-1)])[None], (B, 2, S)),
        "kaux": kaux.reshape(32, 2 * KEYS), "vones": vones,
    }
    arrays = {n: _np.ascontiguousarray(a) for n, a in arrays.items()}
    nc = _bacc.Bacc("TRN2", target_bir_lowering=False, num_devices=1)
    args = [nc.dram_tensor("in_" + n, arrays[n].shape, _mybir.dt.from_np(arrays[n].dtype),
                           kind="ExternalInput").ap() for n in _INS]
    args.append(nc.dram_tensor("outT", (D, B * S), _mybir.dt.float32, kind="ExternalOutput").ap())
    xattn(nc, *args)
    r = _run(nc, [{"in_" + n: arrays[n] for n in _INS}], core_ids=[0])
    return r.results[0]["outT"].T.reshape(B, S, D)
```

```python
import numpy as np
import concourse.bass as bass
from concourse import mybir
from contextlib import ExitStack

B, S, D, C = 16, 256, 320, 512
H, DH = 20, 16
NIP = 4
KEYS = 256
TEXT = KEYS - 2 * NIP
NSP = KEYS - TEXT
GRID = 16
NEG = -10000.0
PAIRS = H // 2
GB = 2
GROUPS = B // GB
GT = GB * S
QUADS = H // 4
OC = -(-H // 8)
SCALE = DH ** -0.5
P = 128
XC, CC = 3, C // P
OT = S // P
MT_ROWS = [128, 128, 64]
VW = 2 * D
AUX = 9
HALF = PAIRS // 2


def xattn(nc, x, xT, ctxT, ctx_sp, bbox, wq, wk, wv, wk_ip, wv_ip, wo, bias, grid, kaux, vones, out):
    f32, f32r = mybir.dt.float32, mybir.dt.float32r
    ALU = mybir.AluOpType
    ACT = mybir.ActivationFunctionType
    AX = mybir.AxisListType

    q_parts = nc.dram_tensor("q_parts", [2, D, B * S], f32, kind="Internal").ap()
    k_parts = nc.dram_tensor("k_parts", [2, D, B * KEYS], f32, kind="Internal").ap()
    v_rows = nc.dram_tensor("v_rows", [B, 2, P, VW], f32, kind="Internal").ap()
    v_sp_rows = nc.dram_tensor("v_sp_rows", [B, NSP, VW], f32, kind="Internal").ap()
    aux_rows = nc.dram_tensor("aux_rows", [B, 32, S], f32, kind="Internal").ap()

    max_rows = nc.dram_tensor("max_rows", [2, 4 * HALF, S], f32, kind="Internal").ap()

    ctx = ExitStack()
    with ctx:
        def sb(name, shape, dt=f32):
            return ctx.enter_context(nc.sbuf_tensor(name, shape, dt))

        def sem(name):
            return ctx.enter_context(nc.semaphore(name))

        q_stack = sb("q_stack", [P, 2, PAIRS * S], f32r)
        k_stack = sb("k_stack", [P, 2, PAIRS * 2 * KEYS], f32r)
        probs = sb("probs", [P, 4, 4 * S])
        o_all = sb("o_all", [P, 4 * QUADS * S])
        o_turned = sb("o_turned", [P, QUADS * 2 * S])
        inv_cols = sb("inv_cols", [P, QUADS, 2 * S // 32])
        v_cur = sb("v_cur", [P, 2, 3, VW])
        x_all = sb("x_all", [P, 6 * S])
        out_sb = sb("out_sb", [P, OT, D])
        wo_sb = sb("wo_sb", [P, OC, D])
        bias_sb = sb("bias_sb", [P, D])
        max_cols = sb("max_cols", [P, 2, 2, 32], f32r)
        row_buf = sb("row_buf", [32, 2, S])

        x_hi = sb("x_hi", [P, XC, GT], f32r)
        x_lo = sb("x_lo", [P, 2, GT], f32r)
        wq_hi = sb("wq_hi", [P, XC, D], f32r)
        wq_lo = sb("wq_lo", [P, XC, D], f32r)
        wk_hl = sb("wk_hl", [P, 2, CC, D], f32r)
        wv_hl = sb("wv_hl", [P, 2, CC, D], f32r)
        qk_out = sb("qk_out", [P, 3, 2, GT], f32r)
        v_out = sb("v_out", [P, 2, VW])
        vsp_out = sb("vsp_out", [P, VW])
        text_mask = sb("text_mask", [P, 1])
        sp_ctx_hl = sb("sp_ctx_hl", [P, 2, CC, P], f32r)
        boxes = sb("boxes", [B, 16])
        zeros = sb("zeros", [B, S], f32r)
        c_hi = k_stack[:, 1, 0:CC * GT].rearrange("p (c n) -> p c n", c=CC)
        c_lo = k_stack[:, 1, CC * GT:2 * CC * GT].rearrange("p (c n) -> p c n", c=CC)
        flat_q = q_stack[:, :, :].rearrange("p a n -> p (a n)")
        wkip_hl = flat_q[:, 0:2 * CC * D].rearrange("p (s c n) -> p s c n", s=2, c=CC)
        wvip_hl = flat_q[:, 2 * CC * D:4 * CC * D].rearrange("p (s c n) -> p s c n", s=2, c=CC)
        flat_o = o_all
        o_raw = o_all[:, 0:2 * QUADS * S].rearrange("p (k n) -> p k n", k=QUADS)
        at = 2 * QUADS * S
        o_norm = o_all[:, at:at + 2 * OC * S].rearrange("p (u c n) -> p u c n", u=2, c=OC)
        o_norm_t = o_all[:, at + 2 * OC * S:at + 3 * OC * S].rearrange("p (c j n) -> p c j n", c=OC, n=32)
        x_raw = flat_o[:, 0:XC * GT].rearrange("p (c n) -> p c n", c=XC)
        c_raw = flat_o[:, XC * GT:(XC + CC) * GT].rearrange("p (c n) -> p c n", c=CC)
        wq_raw = flat_o[:, (XC + CC) * GT:(XC + CC) * GT + XC * D].rearrange("p (c n) -> p c n", c=XC)
        flat_p = probs[:, :, :].rearrange("p a n -> p (a n)")
        wkip_raw, wvip_raw, wk_raw = (
            flat_p[:, i * CC * D:(i + 1) * CC * D].rearrange("p (c n) -> p c n", c=CC) for i in range(3))
        wv_raw = o_turned[:, 0:CC * D].rearrange("p (c n) -> p c n", c=CC)
        sp_raw = o_turned[:, CC * D:CC * D + CC * P].rearrange("p (c n) -> p c n", c=CC)
        ksp_parts = o_turned[:, 0:2 * XC * P].bitcast(f32r).rearrange("p (s m n) -> p s m n", s=2, m=XC)
        kaux_raw = o_turned[96:128, CC * (D + P):CC * (D + P) + 2 * KEYS]
        x_res = x_all[:, 0:2 * OT * D].rearrange("p (u t n) -> p u t n", u=2, t=OT)
        parts = x_all[0:B, :].rearrange("p (k n) -> p k n", k=6)
        grid_sb, inside, covered = parts[:, 0:2, :], parts[:, 2:5, :], parts[:, 5, :]
        mask_out = v_cur[0:B, 0, 0:2, :].rearrange("p k n -> p (k n)").rearrange(
            "p (j n) -> p j n", j=1 + NIP)

        def bank(name, n):
            return ctx.enter_context(nc.psum_tensor(name, [P, n * 512], f32))

        score_t = bank("score_t", 2)
        score_q = bank("score_q", 4)
        pv = bank("pv", 1)
        pj = bank("pj", 1)

        def score_bank(first, n):
            at = 512 * (n % (3 if first else 4))
            return score_q[:, at:at + 512]

        ring = [pj[:, :], pv[:, :], score_t[:, 0:512], score_t[:, 512:1024], score_q[:, 1536:2048]]
        ksp_out = [score_q[:, 0:P], score_q[:, 512:512 + P], score_q[:, 0:P]]
        vsp_psum = score_q[:, 1024:1024 + D]

        ld = {n: sem("loaded_" + n) for n in ("sp", "wkip", "wvip", "wq", "wk", "wv", "small", "boxes")}
        w_high = sem("w_high")
        w_low = sem("w_low")
        x_loaded, c_loaded = sem("x_loaded"), [sem("c_loaded0"), sem("c_loaded1")]
        x_high, c_high = sem("x_high"), sem("c_high")
        x_split, c_split = sem("x_split"), sem("c_split")
        x_tail = sem("x_tail")
        tile_ready = sem("tile_ready")
        hi_done, lo_done = sem("hi_done"), sem("lo_done")
        v_evac = sem("v_evac")
        qk_stored = [sem(f"qk_stored{r}") for r in range(3)]
        v_stored = [sem("v_stored0"), sem("v_stored1")]
        ksp_ready, ksp_hi, ksp_lo = sem("ksp_ready"), sem("ksp_hi"), sem("ksp_lo")
        ksp_stored = sem("ksp_stored")
        vsp_ready, vsp_done = sem("vsp_ready"), sem("vsp_done")
        sp_stored = sem("sp_stored")
        preset, mask_step, mask_done = sem("preset"), sem("mask_step"), sem("mask_done")
        kaux_step = sem("kaux_step")
        aux_stored = sem("aux_stored")
        stacks_set = sem("stacks_set")
        stack_loaded = [[sem(f"stack_loaded{a}{h}") for h in range(2)] for a in range(2)]
        v_loaded = [sem("v_loaded0"), sem("v_loaded1")]
        xr_loaded = [sem("xr_loaded0"), sem("xr_loaded1")]
        sq_ready, max_done = sem("sq_ready"), sem("max_done")
        rows_turned = sem("rows_turned")
        rows_stored = sem("rows_stored")
        rows_loaded = [sem("rows_loaded0"), sem("rows_loaded1")]
        st_ready, exp_done = sem("st_ready"), sem("exp_done")
        pv_ready, o_evac = sem("pv_ready"), sem("o_evac")
        turned, inv_done, scaled = sem("turned"), sem("inv_done"), sem("scaled")
        biased = sem("biased")
        o_added = sem("o_added")
        o_ready = sem("o_ready")
        out_ready, out_done, out_stored = sem("out_ready"), sem("out_done"), sem("out_stored")

        def need(eng, s, value):
            if not isinstance(value, int) or value > 0:
                eng.wait_ge(s, value)

        def values_of(par, kind, h):
            return v_cur[:, par, kind, 2 * DH * h:2 * DH * (h + 1)]

        def halves(row):
            r = row.rearrange("p (h s n) -> p h s n", h=H, s=2)
            return r[:, :, 0, :], r[:, :, 1, :]

        def by_head(row):
            return row.rearrange("p (h n) -> p h n", h=H)

        def q_cols(par, p, a, n):
            return q_stack[:, par, p * S + a:p * S + a + n]

        def k_cols(par, p, head, tile, n):
            at = (2 * p + head) * KEYS + tile * P
            return k_stack[:, par, at:at + n]

        def turned_blocks(k):
            return o_turned[:, k * 2 * S:(k + 1) * 2 * S].rearrange("p (j n) -> p j n", n=32)

        slot = lambda u, p: (PAIRS * u + p) % 4

        def there(b, off=0):
            return not isinstance(b, int) or 0 <= b + off < B

        def batches(eng, body, tail=True):
            for u in range(2):
                body(u, u)
            with eng.Fori(1, B // 2 - 1) as i:
                for u in range(2):
                    body(2 * i + u, u)
            for b in (B - 2, B - 1):
                body(b, b % 2)
            if tail:
                body(B, 0)

        def groups(eng, body):
            body(0)
            with eng.Fori(1, GROUPS - 1) as g:
                body(g)
            body(GROUPS - 1)

        block = ctx.enter_context(nc.Block())

        @block.sync
        def _(sp):
            def rows(a):
                return a.rearrange("(c p) n -> p c n", p=P)

            def load_wq():
                sp.dma_start(wq_raw[:, 0:2, :], rows(wq[0:256, :])).then_inc(ld["wq"], 16)
                for at in (0, 64):
                    sp.dma_start(wq_raw[at:at + 64, 2, :], wq[256:320, :]).then_inc(ld["wq"], 16)

            def load_c(g):
                for h in range(2):
                    need(sp, c_split, 2 * g + h - 1)
                    sp.dma_start(c_raw[:, 2 * h:2 * h + 2, :], rows(ctxT[h * 256:h * 256 + 256, bass.ds(g * GT, GT)]))\
                        .then_inc(c_loaded[h], 16)

            def load_x(g):
                need(sp, x_tail, g)
                cols = bass.ds(g * GT, GT)
                sp.dma_start(x_raw[:, 0:2, :], rows(xT[0:256, cols])).then_inc(x_loaded, 16)
                for at in (0, 64):
                    sp.dma_start(x_raw[at:at + 64, 2, :], xT[256:320, cols]).then_inc(x_loaded, 16)

            def store_qk(g, j):
                m, r, ring = j % 3, MT_ROWS[j % 3], j % 3
                src = qk_out[0:r, ring, :, :].bitcast(f32)
                sp.wait_ge(lo_done, 6 * g + j + 1)
                for s in range(2):
                    if j >= 3:
                        sp.dma_start(q_parts[s, m * P:m * P + r, bass.ds(g * GT, GT)], src[:, s, :])\
                            .then_inc(qk_stored[ring], 16)
                    else:
                        dst = k_parts[s].rearrange("p (b n) -> p b n", n=KEYS)[
                            m * P:m * P + r, bass.ds(g * GB, GB), 0:TEXT]
                        sp.dma_start(dst, src[:, s].rearrange("p (b n) -> p b n", b=GB)[:, :, 0:TEXT])\
                            .then_inc(qk_stored[ring], 16)

            def store_rows(b, h):
                sp.wait_ge(rows_turned, 2 * b + h + 1)
                sp.dma_start(max_rows[h], row_buf[0:4 * HALF, h, :]).then_inc(rows_stored, 16)

            def load_rows(b, u, h):
                sp.wait_ge(rows_stored, 16 * (2 * b + h + 1))
                sp.dma_start(
                    q_stack[96:100, u, h * HALF * S:(h + 1) * HALF * S].rearrange(
                        "p (a n) -> p a n", a=HALF).bitcast(f32),
                    max_rows[h].rearrange("(a k) n -> k a n", k=4)).then_inc(rows_loaded[h], 16)

            def group(g):
                more = not (isinstance(g, int) and g == GROUPS - 1)
                if more:
                    load_c(g + 1)
                else:
                    first_loads()
                store_qk(g, 0)
                store_qk(g, 1)
                store_qk(g, 2)
                if not more:
                    load_stack_q(0, 0, 1)
                for t in range(2 * GB):
                    sp.wait_ge(v_evac, 4 * g + t + 1)
                    dst = v_rows.rearrange("b k p n -> (b k) p n")[bass.ds(2 * GB * g + t, 1), :, :]
                    sp.dma_start(dst.rearrange("a p n -> (a p) n"), v_out[:, t % 2, :])\
                        .then_inc(v_stored[t % 2], 16)
                    if t == 1 and not more:
                        load_stack_k(0, 0, 1)
                if more:
                    load_x(g + 1)
                for j in range(3, 6):
                    store_qk(g, j)
                    if not more and j == 3:
                        store_rows(0, 0)
                        load_stack_q(1, 1, 0)
                        load_rows(0, 0, 0)
                    if not more and j == 4:
                        sp.wait_ge(kaux_step, 2)
                        sp.wait_ge(stacks_set, 2)
                        load_stack_k(1, 1, 0)

            def first_loads():
                for r in range(3):
                    sp.wait_ge(qk_stored[r], 64 * (GROUPS - 2))
                sp.wait_ge(ksp_stored, 96)
                sp.wait_ge(sp_stored, 16)
                sp.wait_ge(aux_stored, 48)
                sp.wait_ge(stacks_set, 1)
                sp.wait_ge(vsp_ready, 1)
                load_stack_q(0, 0, 0)
                load_stack_k(0, 0, 0)

            sp.dma_start(wk_raw, rows(wk)).then_inc(ld["wk"], 16)
            load_c(0)
            sp.dma_start(wv_raw, rows(wv)).then_inc(ld["wv"], 16)
            load_x(0)
            sp.dma_start(wq_raw[:, 0:2, :], rows(wq[0:256, :])).then_inc(ld["wq"], 16)
            for at in (0, 64):
                sp.dma_start(wq_raw[at:at + 64, 2, :], wq[256:320, :]).then_inc(ld["wq"], 16)
            sp.dma_start(sp_raw, rows(ctx_sp)).then_inc(ld["sp"], 16)
            sp.dma_start(wkip_raw, rows(wk_ip)).then_inc(ld["wkip"], 16)
            sp.dma_start(wvip_raw, rows(wv_ip)).then_inc(ld["wvip"], 16)
            sp.dma_start(wo_sb[:, :, :], rows(wo)).then_inc(ld["small"], 16)
            sp.dma_start(bias_sb[:, :], bias.broadcast_to([P, D])).then_inc(ld["small"], 16)

            def load_stack_q(b, u, h):
                ps, n = h * HALF, HALF
                done = stack_loaded[u][h]
                qv = q_stack[:, u, ps * S:(ps + n) * S].rearrange("p (a n) -> p a n", a=n).bitcast(f32)
                for quad, part in enumerate((0, 1, 0)):
                    src = q_parts[part, 32 * ps:32 * (ps + n), bass.ds(b * S, S)].rearrange(
                        "(a r) n -> r a n", r=32)
                    sp.dma_start(qv[32 * quad:32 * quad + 32, :, :], src).then_inc(done, 16)
                src = aux_rows[bass.ds(b, 1), :, :].rearrange("a r n -> (a r) n")
                sp.dma_start(qv[96:128, :, :], src.unsqueeze(1).broadcast_to([32, n, S])).then_inc(done, 16)

            def load_stack_k(b, u, h):
                ps, n = h * HALF, HALF
                kv = k_stack[:, u, ps * 2 * KEYS:(ps + n) * 2 * KEYS].rearrange(
                    "p (a e n) -> p a e n", a=n, e=2).bitcast(f32)
                for quad, part in enumerate((0, 0, 1)):
                    src = k_parts[part, 32 * ps:32 * (ps + n), bass.ds(b * KEYS, KEYS)].rearrange(
                        "(a e r) n -> e r a n", e=2, r=DH)
                    for e in range(2):
                        at = 32 * quad + DH * e
                        sp.dma_start(kv[at:at + DH, :, e, :], src[e]).then_inc(stack_loaded[u][h], 16)

            groups(sp, group)

            def load_values(b, u):
                sp.dma_start(v_cur[:, u, 0:2, :], v_rows[bass.ds(b, 1), :, :, :].rearrange(
                    "a k p n -> (a p) k n")).then_inc(v_loaded[u], 16)
                sp.dma_start(v_cur[P - NSP:P, u, 2, :], v_sp_rows[bass.ds(b, 1), :, :].rearrange(
                    "a p n -> (a p) n")).then_inc(v_loaded[u], 16)

            def load_residual(b, u):
                sp.dma_start(x_res[:, u, :, :], rows(x[bass.ds(b * S, S), :])).then_inc(xr_loaded[u], 16)

            for r in range(2):
                sp.wait_ge(v_stored[r], 32 * (GROUPS - 2))
            sp.wait_ge(mask_done, 1)
            load_values(0, 0)
            for r in range(3):
                sp.wait_ge(qk_stored[r], 64 * GROUPS)
            for r in range(2):
                sp.wait_ge(v_stored[r], 32 * GROUPS)
            sp.wait_ge(kaux_step, 3)
            sp.wait_ge(stacks_set, 3)

            def batch(b, u):
                store_rows(b, 1)
                if there(b, 1):
                    need(sp, st_ready, 2 * PAIRS * b)
                    load_stack_q(b + 1, 1 - u, 1)
                load_rows(b, u, 1)
                if there(b, 1):
                    load_stack_k(b + 1, 1 - u, 1)
                if there(b, -2):
                    store_out(b - 2)
                load_residual(b, u)
                if there(b, 1):
                    need(sp, pv_ready, QUADS * b)
                    load_values(b + 1, 1 - u)
                    store_rows(b + 1, 0)
                if there(b, 2):
                    sp.wait_ge(st_ready, 2 * PAIRS * b + PAIRS)
                    load_stack_q(b + 2, u, 0)
                if there(b, 1):
                    load_rows(b + 1, 1 - u, 0)
                if there(b, 2):
                    load_stack_k(b + 2, u, 0)

            def store_out(b):
                need(sp, out_done, OT * (b + 1))
                sp.dma_start(rows(out[bass.ds(b * S, S), :]), out_sb[:, :, :]).then_inc(out_stored, 16)

            batches(sp, batch, tail=False)
            for b in (B - 2, B - 1):
                store_out(b)
            sp.wait_ge(out_stored, 16 * B)

        @block.gpsimd
        def _(pool):
            pool.dma_start(boxes[:, :], bbox).then_inc(ld["boxes"], 16)
            pool.dma_start(grid_sb, grid).then_inc(ld["boxes"], 16)
            pool.dma_start(kaux_raw, kaux).then_inc(ld["boxes"], 16)
            pool.dma_start(text_mask[:, :], vones).then_inc(ld["boxes"], 16)
            pool.memset(zeros[:, :].bitcast(f32), 0.0).then_inc(preset, 1)
            pool.memset(v_cur[:, :, 2, :], 0.0).then_inc(preset, 1)
            pool.memset(halves(v_out[:, 0, :])[1], 1.0).then_inc(preset, 1)
            pool.memset(halves(vsp_out[:, :])[1], 1.0).then_inc(preset, 1)
            pool.memset(halves(v_out[:, 1, :])[1], 1.0).then_inc(preset, 1)
            pool.memset(max_cols[:, :, :, :].bitcast(f32), 0.0).then_inc(preset, 1)
            pool.memset(k_stack[0:96, 0, :].bitcast(f32), 0.0).then_inc(kaux_step, 1)
            pool.wait_ge(ld["boxes"], 64)
            pool.wait_ge(preset, 6)
            pool.tensor_scalar(halves(v_out[:, 1, :])[1], halves(v_out[:, 1, :])[1], text_mask[:, 0:1], None,
                               ALU.mult).then_inc(preset, 1)
            pool.dma_start(aux_rows[:, 0:4, :], zeros[:, :].bitcast(f32).unsqueeze(1).broadcast_to([B, 4, S])).then_inc(aux_stored, 16)
            pool.dma_start(aux_rows[:, AUX:32, :], zeros[:, :].bitcast(f32).unsqueeze(1).broadcast_to([B, 32 - AUX, S])).then_inc(aux_stored, 16)

            pool.wait_ge(preset, 7)
            pool.wait_ge(kaux_step, 1)
            pool.tensor_copy(
                k_stack[96:128, 0, :].rearrange("p (a n) -> p a n", a=PAIRS),
                kaux_raw.unsqueeze(1).broadcast_to([32, PAIRS, 2 * KEYS])).then_inc(stacks_set, 1)

            for m, r in enumerate(MT_ROWS):
                pool.wait_ge(ksp_lo, m + 1)
                for s in range(2):
                    pool.dma_start(k_parts[s, m * P:m * P + r, :].rearrange("p (b n) -> p b n", b=B)[:, :, TEXT:KEYS],
                                   ksp_parts[0:r, s, m, :].rearrange("p (b n) -> p b n", b=B).bitcast(f32))\
                        .then_inc(ksp_stored, 16)
            pool.wait_ge(vsp_done, 1)
            pool.dma_start(v_sp_rows.rearrange("b p n -> (b p) n"), vsp_out[:, :]).then_inc(sp_stored, 16)
            pool.wait_ge(mask_done, 1)
            pool.dma_start(aux_rows[:, 4:AUX, :], mask_out).then_inc(aux_stored, 16)

            pool.wait_ge(w_low, 3)
            pool.wait_ge(stacks_set, 1)
            pool.memset(o_norm_t[:, :, :, :], 0.0).then_inc(preset, 1)
            pool.wait_ge(tile_ready, 10 * (GROUPS - 1) + 7)
            pool.wait_ge(preset, 8)
            for h in range(2):
                cols = slice(h * HALF * 2 * KEYS, (h + 1) * HALF * 2 * KEYS)
                pool.memset(k_stack[0:96, 1, cols].bitcast(f32), 0.0).then_inc(kaux_step, 1)

            def normalise(b, u):
                pool.wait_ge(xr_loaded[u], 8 * (b - u) + 16)
                pool.tensor_tensor(x_res[:, u, :, :], x_res[:, u, :, :],
                                   bias_sb[:, :].unsqueeze(1).broadcast_to([P, OT, D]), ALU.add).then_inc(biased, 1)
                for k in range(QUADS):
                    n = QUADS * b + k
                    out = turned_blocks(k)[:, :, 0:DH]
                    pool.wait_ge(inv_done, n + 1)
                    pool.tensor_tensor(out, out, inv_cols[:, k, :].unsqueeze(2).broadcast_to(
                        [P, 2 * S // 32, DH]), ALU.mult).then_inc(scaled, 1)
                    pool.wait_ge(scaled, n + 1)
                    need(pool, o_ready, OC * (b - 1) + k // 2 + 1)
                    half = (k % 2) * DH
                    pool.tensor_tensor(o_norm_t[:, k // 2, :, half:half + DH], out[:, 0:S // 32, :],
                                       out[:, S // 32:, :], ALU.add).then_inc(o_added, 1)

            pool.wait_ge(kaux_step, 3)
            pool.wait_ge(ld["small"], 32)
            batches(pool, normalise, tail=False)

        @block.scalar
        def _(act):
            def high(dst, src, loaded, value):
                act.wait_ge(loaded, value)
                nc.scalar.activation(dst, src, ACT.Copy).then_inc(w_high, 1)

            def split_c(g):
                need(act, tile_ready, 10 * (g - 1) + 7)
                for h in range(2):
                    act.wait_ge(c_loaded[h], 16 * (g + 1))
                    nc.scalar.activation(c_hi[:, 2 * h:2 * h + 2], c_raw[:, 2 * h:2 * h + 2], ACT.Copy)\
                        .then_inc(c_high, 1)

            def split_x(g):
                act.wait_ge(x_loaded, 48 * (g + 1))
                need(act, tile_ready, 10 * g)
                nc.scalar.activation(x_hi[:, :, :], x_raw, ACT.Copy).then_inc(x_high, 1)

            def qk_tile(g, j):
                r = MT_ROWS[j % 3]
                n = j if j < 3 else j + 4
                act.wait_ge(tile_ready, 10 * g + n + 1)
                need(act, qk_stored[j % 3], 32 * (2 * g + j // 3))
                nc.scalar.activation(qk_out[0:r, j % 3, 0, :], ring[n % 5][0:r, :], ACT.Copy)\
                    .then_inc(hi_done, 1)

            def v_tile(g, t):
                act.wait_ge(tile_ready, 10 * g + 4 + t)
                need(act, v_stored[t % 2], 16 * (2 * g + t // 2))
                out = halves(v_out[:, t % 2, :])[0]
                src = by_head(ring[(3 + t) % 5][:, 0:D])
                if t % 2:
                    nc.scalar.activation(out, src, ACT.Copy, scale=text_mask[:, 0:1]).then_inc(v_evac, 1)
                else:
                    nc.scalar.activation(out, src, ACT.Copy).then_inc(v_evac, 1)

            def group(g):
                first, last = (isinstance(g, int) and g == n for n in (0, GROUPS - 1))
                qk_tile(g, 0)
                split_x(g)
                if first:
                    high(wv_hl[:, 0], wv_raw, ld["wv"], 16)
                    high(wq_hi[:, :, :], wq_raw, ld["wq"], 48)
                qk_tile(g, 1)
                qk_tile(g, 2)
                if first:
                    high(sp_ctx_hl[:, 0], sp_raw, ld["sp"], 16)
                    high(wkip_hl[:, 0], wkip_raw, ld["wkip"], 16)
                    high(wvip_hl[:, 0], wvip_raw, ld["wvip"], 16)
                    act.wait_ge(preset, 7)
                for t in range(4):
                    v_tile(g, t)
                if not last:
                    split_c(g + 1)
                for j in range(3, 6):
                    qk_tile(g, j)
                    if last and j < 5:
                        act.wait_ge(stacks_set, j - 2)
                        cols = slice((j - 3) * HALF * 2 * KEYS, (j - 2) * HALF * 2 * KEYS)
                        nc.scalar.activation(
                            k_stack[96:128, 1, cols].rearrange("p (a n) -> p a n", a=HALF),
                            kaux_raw.unsqueeze(1).broadcast_to([32, HALF, 2 * KEYS]), ACT.Copy)\
                            .then_inc(stacks_set, 1)
                if first:
                    for m, r in enumerate(MT_ROWS):
                        act.wait_ge(ksp_ready, m + 1)
                        nc.scalar.activation(ksp_parts[0:r, 0, m, :], ksp_out[m][0:r, :], ACT.Copy)\
                            .then_inc(ksp_hi, 1)
                    act.wait_ge(vsp_ready, 1)
                    nc.scalar.activation(halves(vsp_out[:, :])[0], by_head(vsp_psum), ACT.Copy).then_inc(vsp_done, 1)

            high(wk_hl[:, 0], wk_raw, ld["wk"], 16)
            split_c(0)
            groups(act, group)

            def evacuate(b, u, k):
                n = QUADS * b + k
                act.wait_ge(pv_ready, n + 1)
                need(act, turned, n + 1 - QUADS)
                nc.scalar.activation(o_raw[:, k, :], pv[:, :], ACT.Copy)\
                    .then_inc(o_evac, 1)

            def batch(b, u):
                for p in range(PAIRS):
                    for e in range(2):
                        if there(b):
                            act.wait_ge(st_ready, 2 * (PAIRS * b + p) + e + 1)
                            if p % 2 == 0 and e == 0:
                                need(act, pv_ready, QUADS * b + (p - 4) // 2 + 1)
                            nc.scalar.activation(probs[:, slot(u, p), 2 * S * e:2 * S * (e + 1)],
                                                 score_t[:, 512 * e:512 * e + 512], ACT.Exp, scale=SCALE)\
                                .then_inc(exp_done, 1)
                        if e == 1:
                            for k, off in EVACUATE.get(p, ()):
                                if there(b, off):
                                    evacuate(b + off, (u + off) % 2, k)

            batches(act, batch)

        @block.vector
        def _(dve):
            steps = [0]

            def then(ins):
                steps[0] += 1
                ins.then_inc(mask_step, 1)
                dve.wait_ge(mask_step, steps[0])

            def mask():
                dve.wait_ge(ld["boxes"], 64)
                gx, gy = grid_sb[:, 0, :], grid_sb[:, 1, :]
                for j in range(NIP):
                    side = lambda c: boxes[:, 4 * j + c:4 * j + c + 1]
                    at = inside_j(j)
                    then(nc.vector.tensor_scalar(at, gx, side(0), None, ALU.is_ge))
                    for g, c, op in ((gx, 2, ALU.is_le), (gy, 1, ALU.is_ge), (gy, 3, ALU.is_le)):
                        then(nc.vector.scalar_tensor_tensor(out=at, in0=g, scalar=side(c), in1=at,
                                                            op0=op, op1=ALU.mult))
                    then(nc.vector.tensor_scalar(mask_out[:, 1 + j, :], at, -NEG / SCALE, NEG / SCALE,
                                                 ALU.mult, ALU.add))
                    if j == 0:
                        then(nc.vector.tensor_copy(covered, at))
                    else:
                        then(nc.vector.tensor_tensor(covered, covered, at, ALU.max))
                nc.vector.tensor_scalar(mask_out[:, 0, :], covered, NEG / SCALE, None, ALU.mult)\
                    .then_inc(mask_done, 1)

            def inside_j(j):
                return inside[:, j % 3, :]

            n_low = [0]

            def low(dst, raw, hi):
                n_low[0] += 1
                dve.wait_ge(w_high, n_low[0])
                nc.vector.tensor_tensor(dst, raw, hi.bitcast(f32), ALU.subtract).then_inc(w_low, 1)

            def split_c(g):
                for h in range(2):
                    cc = slice(2 * h, 2 * h + 2)
                    dve.wait_ge(c_high, 2 * g + h + 1)
                    nc.vector.tensor_tensor(c_lo[:, cc], c_raw[:, cc], c_hi[:, cc].bitcast(f32),
                                            ALU.subtract).then_inc(c_split, 1)

            def split_x(g):
                dve.wait_ge(x_high, g + 1)
                nc.vector.tensor_tensor(x_lo[:, :, :], x_raw[:, 0:2, :], x_hi[:, 0:2, :].bitcast(f32),
                                        ALU.subtract).then_inc(x_split, 1)
                nc.vector.tensor_tensor(x_hi[64:128, 2, :], x_raw[64:128, 2, :],
                                        x_hi[64:128, 2, :].bitcast(f32), ALU.subtract).then_inc(x_tail, 1)

            def qk_tile(g, j):
                r = MT_ROWS[j % 3]
                n = j if j < 3 else j + 4
                dve.wait_ge(hi_done, 6 * g + j + 1)
                nc.vector.tensor_tensor(qk_out[0:r, j % 3, 1, :], ring[n % 5][0:r, :],
                                        qk_out[0:r, j % 3, 0, :].bitcast(f32), ALU.subtract)\
                    .then_inc(lo_done, 1)

            def maxima(b, p, t):
                h, at = p // HALF, 4 * (p % HALF)
                if at == 0 and t == 0:
                    need(dve, rows_turned, 2 * b + h - 1)
                dve.wait_ge(sq_ready, 2 * (PAIRS * b + p) + t + 1)
                both = score_bank(isinstance(b, int) and b == 0, 2 * p + t).rearrange("p (e n) -> p e n", e=2)
                nc.vector.tensor_reduce(out=max_cols[:, h, t, at:at + 2], in_=both[:, :, 0:TEXT],
                                        op=ALU.max, axis=AX.X, negate=True)
                nc.vector.tensor_reduce(out=max_cols[:, h, t, at + 2:at + 4], in_=both[:, :, TEXT:KEYS],
                                        op=ALU.max, axis=AX.X, negate=True).then_inc(max_done, 1)

            def turn(b, h):
                dve.wait_ge(max_done, 2 * (PAIRS * b + HALF * (h + 1)))
                need(dve, rows_stored, 16 * (2 * b + h - 1))
                to = row_buf[:, h, :].rearrange("r (t i n) -> r t i n", t=2, i=4)
                for i in range(4):
                    last = nc.vector.transpose(to[:, :, i, :], max_cols[32 * i:32 * i + 32, h, :, :].bitcast(f32))
                last.then_inc(rows_turned, 1)

            def first_maxima(tile):
                for p in FIRST_SCORES.get(tile, ()):
                    for t in range(2):
                        maxima(0, p, t)
                    if p % HALF == HALF - 1:
                        turn(0, p // HALF)

            def group(g):
                first, last = (isinstance(g, int) and g == n for n in (0, GROUPS - 1))
                qk_tile(g, 0)
                split_x(g)
                if first:
                    low(wv_hl[:, 1], wv_raw, wv_hl[:, 0])
                    low(wq_lo[:, :, :], wq_raw, wq_hi[:, :, :])
                qk_tile(g, 1)
                qk_tile(g, 2)
                if first:
                    low(sp_ctx_hl[:, 1], sp_raw, sp_ctx_hl[:, 0])
                    low(wkip_hl[:, 1], wkip_raw, wkip_hl[:, 0])
                    low(wvip_hl[:, 1], wvip_raw, wvip_hl[:, 0])
                if last:
                    dve.wait_ge(preset, 7)
                    for n in range(3, 7):
                        first_maxima(n)
                else:
                    split_c(g + 1)
                for j in range(3, 6):
                    qk_tile(g, j)
                    if last:
                        first_maxima(j + 4)
                if first:
                    for m, r in enumerate(MT_ROWS):
                        dve.wait_ge(ksp_hi, m + 1)
                        nc.vector.tensor_tensor(ksp_parts[0:r, 1, m, :], ksp_out[m][0:r, :],
                                                ksp_parts[0:r, 0, m, :].bitcast(f32), ALU.subtract)\
                            .then_inc(ksp_lo, 1)
                    mask()

            low(wk_hl[:, 1], wk_raw, wk_hl[:, 0])
            split_c(0)
            groups(dve, group)

            def invert(b, k):
                n = QUADS * b + k
                dve.wait_ge(o_evac, n + 1)
                need(dve, o_added, n + 1 - QUADS)
                nc.vector.transpose(turned_blocks(k), o_raw[:, k, :].rearrange("p (j n) -> p j n", n=32))\
                    .then_inc(turned, 1)
                dve.wait_ge(turned, n + 1)
                nc.vector.reciprocal(inv_cols[:, k, :], turned_blocks(k)[:, :, DH]).then_inc(inv_done, 1)

            def turn_back(b, u, c):
                dve.wait_ge(o_added, QUADS * b + min(2 * c + 2, QUADS))
                if c == 0:
                    need(dve, out_ready, OT * (b - 1))
                nc.vector.transpose(o_norm[:, u, c, :].rearrange("p (j n) -> p j n", n=32),
                                    o_norm_t[:, c, :, :]).then_inc(o_ready, 1)

            def finish(b, u, t):
                dve.wait_ge(out_ready, OT * b + t + 1)
                if t == 0:
                    need(dve, out_stored, 16 * b)
                    dve.wait_ge(biased, b + 1)
                nc.vector.tensor_tensor(out_sb[:, t, :], pj[:, 0:D], x_res[:, u, t, :], ALU.add)\
                    .then_inc(out_done, 1)

            def batch(b, u):
                for p in range(PAIRS):
                    for t in range(2):
                        if there(b, 1) and there(b):
                            maxima(b + 1, p, t)
                        if t == 0:
                            for c, off in TURN_BACK.get(p, ()):
                                if there(b, off):
                                    turn_back(b + off, (u + off) % 2, c)
                            for k, off in INVERT.get(p, ()):
                                if there(b, off):
                                    invert(b + off, k)
                            for m, off in FINISH.get(p, ()):
                                if there(b, off):
                                    finish(b + off, (u + off) % 2, m)
                    if p % HALF == HALF - 1 and there(b, 1) and there(b):
                        turn(b + 1, p // HALF)

            batches(dve, batch)
            finish(B - 1, 1, OT - 1)
        @block.tensor
        def _(pe):
            mm = nc.tensor.matmul

            def three(out, w_hi, w_lo, x_hi_, x_lo_, start, stop):
                mm(out, w_hi, x_hi_, start=start, stop=False)
                mm(out, w_lo, x_hi_, start=False, stop=False)
                return mm(out, w_hi, x_lo_, start=False, stop=stop)

            def k_tile(g, m, out):
                r, cols = MT_ROWS[m], slice(m * P, m * P + MT_ROWS[m])
                for c in range(CC):
                    if m == 0 and c % 2 == 0:
                        pe.wait_ge(c_split, 2 * g + c // 2 + 1)
                    last = three(out[0:r, :], wk_hl[:, 0, c, cols], wk_hl[:, 1, c, cols], c_hi[:, c, :],
                                 c_lo[:, c, :], c == 0, c == CC - 1)
                last.then_inc(tile_ready, 1)

            def v_tile(g, t, out):
                keys = slice(t * P, t * P + P)
                for c in range(CC):
                    last = three(out[:, 0:D], c_hi[:, c, keys], c_lo[:, c, keys],
                                 wv_hl[:, 0, c, :], wv_hl[:, 1, c, :], c == 0, c == CC - 1)
                last.then_inc(tile_ready, 1)

            def q_tile(g, m, out):
                r, cols = MT_ROWS[m], slice(m * P, m * P + MT_ROWS[m])
                for c in range(2):
                    three(out[0:r, :], wq_hi[:, c, cols], wq_lo[:, c, cols], x_hi[:, c, :], x_lo[:, c, :],
                          c == 0, False)
                mm(out[0:r, :], wq_hi[:, 2, cols], x_hi[:, 2, :], start=False, stop=False)
                mm(out[0:r, :], wq_lo[:, 2, cols], x_hi[:, 2, :], start=False, stop=True)\
                    .then_inc(tile_ready, 1)

            def query_scores(b, u, p, t):
                first = isinstance(b, int) and b == 0
                if p % HALF == 0 and t == 0:
                    pe.wait_ge(stack_loaded[u][p // HALF], 80 * (b - u) + 160)
                n = 2 * (PAIRS * b + p) + t
                if isinstance(b, int) and b == 1 and p < 2:
                    pe.wait_ge(max_done, 2 * PAIRS)
                else:
                    need(pe, max_done, n - (2 if first else 3))
                mm(score_bank(first, 2 * p + t), q_cols(u, p, t * P, P),
                   k_cols(u, p, 0, 0, 2 * KEYS), start=True, stop=True).then_inc(sq_ready, 1)

            def group(g):
                first = isinstance(g, int) and g == 0
                for n in range(10):
                    if n == 7:
                        pe.wait_ge(x_tail, g + 1)
                    if first and n in (0, 3, 7):
                        pe.wait_ge(w_low, {0: 1, 3: 2, 7: 3}[n])
                    left, count = [(v_evac, 4 * g - 1), (v_evac, 4 * g), (lo_done, 6 * g - 2),
                                   (lo_done, 6 * g - 1), (lo_done, 6 * g), (lo_done, 6 * g + 1),
                                   (lo_done, 6 * g + 2), (lo_done, 6 * g + 3), (v_evac, 4 * g + 1),
                                   (v_evac, 4 * g + 2)][n]
                    need(pe, left, count)
                    out = ring[n % 5]
                    if n < 3:
                        k_tile(g, n, out)
                    elif n < 7:
                        v_tile(g, n - 3, out)
                    else:
                        q_tile(g, n - 7, out)
                    if isinstance(g, int) and g == GROUPS - 1:
                        for p in FIRST_SCORES.get(n, ()):
                            for t in range(2):
                                query_scores(0, 0, p, t)
                if first:
                    special()

            def special():
                pe.wait_ge(w_low, 5)
                for m, r in enumerate(MT_ROWS):
                    if m == 2:
                        pe.wait_ge(ksp_lo, 1)
                    for c in range(CC):
                        last = three(ksp_out[m][0:r, :], wkip_hl[:, 0, c, m * P:m * P + r],
                                     wkip_hl[:, 1, c, m * P:m * P + r], sp_ctx_hl[:, 0, c, :],
                                     sp_ctx_hl[:, 1, c, :], c == 0, c == CC - 1)
                    last.then_inc(ksp_ready, 1)
                pe.wait_ge(w_low, 6)
                for c in range(CC):
                    last = three(vsp_psum, sp_ctx_hl[:, 0, c, :], sp_ctx_hl[:, 1, c, :],
                                 wvip_hl[:, 0, c, :], wvip_hl[:, 1, c, :], c == 0, c == CC - 1)
                last.then_inc(vsp_ready, 1)

            groups(pe, group)

            def key_scores(b, u, p, e):
                if p % HALF == 0 and e == 0:
                    pe.wait_ge(rows_loaded[p // HALF], 16 * (b + 1))
                need(pe, exp_done, 2 * (PAIRS * b + p) + e - 1)
                for t in range(2):
                    last = mm(score_t[:, 512 * e + S * t:512 * e + S * t + S], k_cols(u, p, e, t, P),
                              q_cols(u, p, 0, S), start=True, stop=True)
                last.then_inc(st_ready, 1)

            def values(b, u, k, kinds):
                if k == 0 and 0 in kinds:
                    pe.wait_ge(v_loaded[u], 16 * (b - u) + 32)
                if 0 in kinds:
                    need(pe, o_evac, QUADS * b + k)
                    pe.wait_ge(exp_done, 2 * PAIRS * b + 4 * (k + 1))
                for kind in kinds:
                    tile = min(kind, 1)
                    for t in range(4):
                        a = (t % 2) * 2 * S + tile * S
                        at = S if kind == 2 else 0
                        last = mm(pv[32 * t:32 * t + 32, at:at + S], values_of(u, kind, 4 * k + t),
                                  probs[:, slot(u, 2 * k + t // 2), a:a + S],
                                  start=kind != 1, stop=kind != 0)
                if 2 in kinds:
                    last.then_inc(pv_ready, 1)

            def project_out(b, u, t, c):
                if t == 0:
                    pe.wait_ge(o_ready, OC * b + c + 1)
                if c == 0:
                    need(pe, out_done, OT * b + t)
                last = mm(pj[:, 0:D], o_norm[:, u, c, t * P:t * P + P], wo_sb[:, c, :],
                          start=c == 0, stop=c == OC - 1)
                if c == OC - 1:
                    last.then_inc(out_ready, 1)

            pe.wait_ge(ld["small"], 32)
            pe.wait_ge(v_evac, 4 * GROUPS)
            pe.wait_ge(lo_done, 6 * GROUPS)
            def batch(b, u):
                for p in range(PAIRS):
                    for half in range(2):
                        if there(b):
                            key_scores(b, u, p, half)
                        if there(b) and there(b, 1):
                            query_scores(b + 1, 1 - u, p, half)
                        if half == (p + 1) % 2:
                            for k, kinds, off in VALUES.get(p, ()):
                                if there(b, off):
                                    values(b + off, (u + off) % 2, k, kinds)
                        if half == 1:
                            for m, k in OUT.get(p, ()):
                                if there(b, -1):
                                    project_out(b - 1, 1 - u, m, k)

            batches(pe, batch)


VALUES = {p: [((p - 2) // 2, (0, 1) if p % 2 == 0 else (2,), 0)] for p in range(2, PAIRS)}
VALUES[0], VALUES[1] = [(QUADS - 1, (0, 1), -1)], [(QUADS - 1, (2,), -1)]
EVACUATE = {3: [(0, 0)], 5: [(1, 0)], 7: [(2, 0)], 9: [(3, 0)], 1: [(4, -1)]}
INVERT = {4: [(0, 0)], 6: [(1, 0)], 8: [(2, 0)], 0: [(3, -1)], 2: [(4, -1)]}
TURN_BACK = {8: [(0, 0)], 2: [(1, -1)], 4: [(2, -1)]}
OUT = {3: [(0, 0), (0, 1)], 5: [(0, 2)], 7: [(1, 0), (1, 1)], 9: [(1, 2)]}
FINISH = {6: [(0, -1)], 0: [(1, -2)]}


FIRST_SCORES = {3: [0, 1], 4: [2], 5: [3], 6: [4], 7: [5, 6], 8: [7], 9: [8, 9]}

_INS = ["x", "xT", "ctxT", "ctx_sp", "bbox", "wq", "wk", "wv", "wk_ip", "wv_ip", "wo", "bias",
        "grid", "kaux", "vones"]


def kernel(x, ctx_2048, fside_Bx4x4_0, L0_xattn_w_q, L0_xattn_w_k, L0_xattn_w_v, L0_xattn_w_k_ip,
           L0_xattn_w_v_ip, L0_xattn_w_out, L0_xattn_b_out):
    import numpy as _np
    import concourse.bacc as _bacc
    from concourse import mybir as _mybir
    from concourse.bass_utils import run_bass_kernel_spmd as _run

    f = _np.float32
    ctx = _np.asarray(ctx_2048)
    wo = _np.zeros((2 * OC, 4, DH, D), f)
    wo[:QUADS] = _np.asarray(L0_xattn_w_out).reshape(QUADS, 4, DH, D)
    wo = wo.reshape(OC, 2, 4, DH, D).transpose(0, 2, 1, 3, 4)
    line = _np.arange(GRID, dtype=f) * f(1.0 / (GRID - 1))
    line[-1] = 1
    gy, gx = _np.meshgrid(line, line, indexing="ij")
    kaux = _np.zeros((32, 2, KEYS), f)
    for e in range(2):
        kaux[e, e, :TEXT] = 1
        kaux[2 + e, e, TEXT:] = 1
    kaux[4, :, TEXT:TEXT + NIP] = 1
    for j in range(NIP):
        kaux[5 + j, :, TEXT + NIP + j] = 1
    vones = _np.ones((P, 1), f)
    vones[P - NSP:] = 0
    arrays = {
        "x": _np.asarray(x).reshape(B * S, D), "xT": _np.asarray(x).reshape(B * S, D).T,
        "ctxT": ctx.reshape(B * KEYS, C).T,
        "ctx_sp": ctx[:, TEXT:].reshape(B * NSP, C).T,
        "bbox": _np.asarray(fside_Bx4x4_0).reshape(B, 16),
        "wq": _np.asarray(L0_xattn_w_q), "wk": _np.asarray(L0_xattn_w_k),
        "wv": _np.asarray(L0_xattn_w_v), "wk_ip": _np.asarray(L0_xattn_w_k_ip),
        "wv_ip": _np.asarray(L0_xattn_w_v_ip), "wo": wo.reshape(OC * P, D),
        "bias": _np.asarray(L0_xattn_b_out).reshape(1, D),
        "grid": _np.broadcast_to(_np.stack([gx.reshape(-1), gy.reshape(-1)])[None], (B, 2, S)),
        "kaux": kaux.reshape(32, 2 * KEYS), "vones": vones,
    }
    arrays = {n: _np.ascontiguousarray(a) for n, a in arrays.items()}
    nc = _bacc.Bacc("TRN2", target_bir_lowering=False, num_devices=1)
    args = [nc.dram_tensor("in_" + n, arrays[n].shape, _mybir.dt.from_np(arrays[n].dtype),
                           kind="ExternalInput").ap() for n in _INS]
    args.append(nc.dram_tensor("out", (B * S, D), _mybir.dt.float32, kind="ExternalOutput").ap())
    xattn(nc, *args)
    r = _run(nc, [{"in_" + n: arrays[n] for n in _INS}], core_ids=[0])
    return r.results[0]["out"].reshape(B, S, D)
```
